# Optimizing a Trainium2 kernel written in Bass

```python
import numpy as np
import jax
import jax.numpy as jnp

def _softmax(x, axis=-1):
    return jax.nn.softmax(x, axis=axis)

def _gelu(x):
    return jax.nn.gelu(x, approximate=True)

def _silu(x):
    return jax.nn.silu(x)

def _sigmoid(x):
    return jax.nn.sigmoid(x)

def _layernorm(x, axis=-1, eps=1e-05):
    m = jnp.mean(x, axis=axis, keepdims=True)
    v = jnp.var(x, axis=axis, keepdims=True)
    return (x - m) / jnp.sqrt(v + eps)

def _scatter_add(tgt, idx, src, axis=0):
    return tgt.at[idx].add(src)

def _segment_sum(src, seg, n):
    return jax.ops.segment_sum(src, seg, n)
kernel_name = 'mk_audio_tower_d2_tok_audfeat1024_r4_7a572a'

def setup_inputs(seed: int=0):
    np.random.seed(seed)
    _w = jnp.asarray

    def _rec_inputs():
        import jax
        import jax.numpy as jnp
        _rk = jax.random.key(seed)
        x = 7.22013e-05 + 1.00017 * jax.random.normal(jax.random.fold_in(_rk, 1), (32, 256, 256), jnp.float32)
        return x
    x = _rec_inputs()

    def _L0_tok_setup():
        import jax, jax.numpy as jnp
        import numpy as np
        DIM = 256
        NUM_HEADS = 16
        HEAD_DIM = DIM // NUM_HEADS
        SCALE = DIM ** (-0.5)
        key = jax.random.key(seed)
        k1, k2, k3 = jax.random.split(key, 3)
        B, S = (4, 512)
        inputs = jax.random.normal(k1, (B, S, DIM), dtype=jnp.float32)
        Wqkv = jax.random.normal(k2, (3 * DIM, DIM), dtype=jnp.float32) * DIM ** (-0.5)
        Wproj = jax.random.normal(k3, (DIM, DIM), dtype=jnp.float32) * DIM ** (-0.5)
        return {'inputs': inputs, 'Wqkv': Wqkv, 'Wproj': Wproj}
    _L0_tok_all = _L0_tok_setup()
    _L0_tok_in = {k: v for k, v in _L0_tok_all.items() if k in ('Wqkv', 'Wproj')}
    del _L0_tok_all

    def _L0_attn_setup():
        import jax, jax.numpy as jnp
        import numpy as np
        from jax import lax
        D_MODEL, D_CONV, EXPAND = (256, 4, 2)
        D_INNER = D_MODEL * EXPAND
        B, N = (4, 512)
        key = jax.random.key(seed)
        ks = jax.random.split(key, 10)
        s = 0.02
        return {'x': jax.random.normal(ks[0], (B, N, D_MODEL), jnp.float32), 'W_in': jax.random.normal(ks[1], (D_MODEL, 2 * D_INNER), jnp.float32) * s, 'b_in': jnp.zeros((2 * D_INNER,), jnp.float32), 'conv_w': jax.random.normal(ks[2], (D_INNER, 1, D_CONV), jnp.float32) * 0.2, 'conv_b': jnp.zeros((D_INNER,), jnp.float32), 'W_bc': jax.random.normal(ks[3], (D_INNER, 2 * D_INNER), jnp.float32) * s, 'b_bc': jnp.zeros((2 * D_INNER,), jnp.float32), 'log_decay': jnp.zeros((D_INNER,), jnp.float32), 'W_out': jax.random.normal(ks[4], (D_INNER, D_MODEL), jnp.float32) * s, 'b_out': jnp.zeros((D_MODEL,), jnp.float32)}
    _L0_attn_all = _L0_attn_setup()
    _L0_attn_in = {k: v for k, v in _L0_attn_all.items() if k in ('W_in', 'b_in', 'conv_w', 'conv_b', 'W_bc', 'b_bc', 'log_decay', 'W_out', 'b_out')}
    del _L0_attn_all

    def _L0_ffn_setup():
        import jax, jax.numpy as jnp
        import numpy as np
        B, S, D, F, O = (4, 512, 256, 1024, 256)
        E, NS, K = (4, 2, 2)
        key = jax.random.key(seed)
        ks = jax.random.split(key, 6)

        def w(k, shape, fan_in):
            return jax.random.normal(k, shape, jnp.float32) * fan_in ** (-0.5)
        return {'x': jax.random.normal(ks[0], (B, S, D), jnp.float32), 'gate_w': w(ks[1], (D, E), D), 'gate_b': jnp.zeros((E,), jnp.float32), 'sw1': w(ks[2], (NS, D, F), D), 'sb1': jnp.zeros((NS, F), jnp.float32), 'sw2': w(ks[3], (NS, F, O), F), 'sb2': jnp.zeros((NS, O), jnp.float32), 'rw1': w(ks[4], (E, D, F), D), 'rb1': jnp.zeros((E, F), jnp.float32), 'rw2': w(ks[5], (E, F, O), F), 'rb2': jnp.zeros((E, O), jnp.float32)}
    _L0_ffn_all = _L0_ffn_setup()
    _L0_ffn_in = {k: v for k, v in _L0_ffn_all.items() if k in ('gate_w', 'gate_b', 'sw1', 'sb1', 'sw2', 'sb2', 'rw1', 'rb1', 'rw2', 'rb2')}
    del _L0_ffn_all

    def _L1_attn_setup():
        import jax, jax.numpy as jnp
        import numpy as np
        import math
        D_MODEL = 256
        N_HEADS = 16
        D_K = D_MODEL // N_HEADS
        MAX_REL = 32
        key = jax.random.key(seed)
        ks = jax.random.split(key, 8)
        B, S = (8, 256)
        x = jax.random.normal(ks[0], (B, S, D_MODEL), dtype=jnp.float32)
        scale = 1.0 / math.sqrt(D_MODEL)
        Wq = jax.random.normal(ks[1], (D_MODEL, D_MODEL), dtype=jnp.float32) * scale
        Wk = jax.random.normal(ks[2], (D_MODEL, D_MODEL), dtype=jnp.float32) * scale
        Wv = jax.random.normal(ks[3], (D_MODEL, D_MODEL), dtype=jnp.float32) * scale
        Wo = jax.random.normal(ks[4], (D_MODEL, D_MODEL), dtype=jnp.float32) * scale
        b_o = jnp.zeros((D_MODEL,), dtype=jnp.float32)
        rel_k_emb = jax.random.normal(ks[5], (2 * MAX_REL + 1, D_K), dtype=jnp.float32) * 0.02
        rel_v_emb = jax.random.normal(ks[6], (2 * MAX_REL + 1, D_K), dtype=jnp.float32) * 0.02
        return {'x': x, 'Wq': Wq, 'Wk': Wk, 'Wv': Wv, 'Wo': Wo, 'b_o': b_o, 'rel_k_emb': rel_k_emb, 'rel_v_emb': rel_v_emb}
    _L1_attn_all = _L1_attn_setup()
    _L1_attn_in = {k: v for k, v in _L1_attn_all.items() if k in ('Wq', 'Wk', 'Wv', 'Wo', 'b_o', 'rel_k_emb', 'rel_v_emb')}
    del _L1_attn_all

    def _L1_ffn_setup():
        import jax, jax.numpy as jnp
        import numpy as np
        NUM_EXPERTS = 8
        TOP_K = 2
        key = jax.random.key(seed)
        ks = jax.random.split(key, 4)
        B, S, H, F = (4, 1024, 256, 1024)
        x = jax.random.normal(ks[0], (B, S, H), dtype=jnp.float32)
        router_w = jax.random.normal(ks[1], (H, NUM_EXPERTS), dtype=jnp.float32) * 0.02
        w1 = jax.random.normal(ks[2], (H, F), dtype=jnp.float32) * 0.02
        b1 = jnp.zeros((F,), dtype=jnp.float32)
        w2 = jax.random.normal(ks[3], (F, H), dtype=jnp.float32) * 0.02
        b2 = jnp.zeros((H,), dtype=jnp.float32)
        return {'x': x, 'router_w': router_w, 'w1': w1, 'b1': b1, 'w2': w2, 'b2': b2}
    _L1_ffn_all = _L1_ffn_setup()
    _L1_ffn_in = {k: v for k, v in _L1_ffn_all.items() if k in ('router_w', 'w1', 'b1', 'w2', 'b2')}
    del _L1_ffn_all
    return {'x': x, 'L0_tok_Wqkv': _L0_tok_in['Wqkv'], 'L0_tok_Wproj': _L0_tok_in['Wproj'], 'L0_attn_W_in': _L0_attn_in['W_in'], 'L0_attn_b_in': _L0_attn_in['b_in'], 'L0_attn_conv_w': _L0_attn_in['conv_w'], 'L0_attn_conv_b': _L0_attn_in['conv_b'], 'L0_attn_W_bc': _L0_attn_in['W_bc'], 'L0_attn_b_bc': _L0_attn_in['b_bc'], 'L0_attn_log_decay': _L0_attn_in['log_decay'], 'L0_attn_W_out': _L0_attn_in['W_out'], 'L0_attn_b_out': _L0_attn_in['b_out'], 'L0_ffn_gate_w': _L0_ffn_in['gate_w'], 'L0_ffn_gate_b': _L0_ffn_in['gate_b'], 'L0_ffn_sw1': _L0_ffn_in['sw1'], 'L0_ffn_sb1': _L0_ffn_in['sb1'], 'L0_ffn_sw2': _L0_ffn_in['sw2'], 'L0_ffn_sb2': _L0_ffn_in['sb2'], 'L0_ffn_rw1': _L0_ffn_in['rw1'], 'L0_ffn_rb1': _L0_ffn_in['rb1'], 'L0_ffn_rw2': _L0_ffn_in['rw2'], 'L0_ffn_rb2': _L0_ffn_in['rb2'], 'L1_attn_Wq': _L1_attn_in['Wq'], 'L1_attn_Wk': _L1_attn_in['Wk'], 'L1_attn_Wv': _L1_attn_in['Wv'], 'L1_attn_Wo': _L1_attn_in['Wo'], 'L1_attn_b_o': _L1_attn_in['b_o'], 'L1_attn_rel_k_emb': _L1_attn_in['rel_k_emb'], 'L1_attn_rel_v_emb': _L1_attn_in['rel_v_emb'], 'L1_ffn_router_w': _L1_ffn_in['router_w'], 'L1_ffn_w1': _L1_ffn_in['w1'], 'L1_ffn_b1': _L1_ffn_in['b1'], 'L1_ffn_w2': _L1_ffn_in['w2'], 'L1_ffn_b2': _L1_ffn_in['b2']}

def reference(x, L0_tok_Wqkv, L0_tok_Wproj, L0_attn_W_in, L0_attn_b_in, L0_attn_conv_w, L0_attn_conv_b, L0_attn_W_bc, L0_attn_b_bc, L0_attn_log_decay, L0_attn_W_out, L0_attn_b_out, L0_ffn_gate_w, L0_ffn_gate_b, L0_ffn_sw1, L0_ffn_sb1, L0_ffn_sw2, L0_ffn_sb2, L0_ffn_rw1, L0_ffn_rb1, L0_ffn_rw2, L0_ffn_rb2, L1_attn_Wq, L1_attn_Wk, L1_attn_Wv, L1_attn_Wo, L1_attn_b_o, L1_attn_rel_k_emb, L1_attn_rel_v_emb, L1_ffn_router_w, L1_ffn_w1, L1_ffn_b1, L1_ffn_w2, L1_ffn_b2):
    import jax
    import jax.numpy as jnp

    def _L0_tok_ref(inputs, Wqkv, Wproj):
        import jax, jax.numpy as jnp
        import numpy as np
        DIM = 256
        NUM_HEADS = 16
        HEAD_DIM = DIM // NUM_HEADS
        SCALE = DIM ** (-0.5)
        B = inputs.shape[0]
        qkv = inputs @ Wqkv.T
        qkv = qkv.reshape(B, -1, 4, NUM_HEADS, HEAD_DIM)
        qkv = qkv.transpose(2, 0, 3, 1, 4)
        q, k, v = (qkv[0], qkv[1], qkv[2])
        attn = jnp.einsum('bhqd,bhkd->bhqk', q, k) * SCALE
        attn = jax.nn.softmax(attn, axis=-1)
        x = jnp.einsum('bhqk,bhkd->bhqd', attn, v)
        x = x.transpose(0, 2, 1, 3).reshape(B, -1, DIM)
        return x @ Wproj.T

    def _L0_attn_ref(x, W_in, b_in, conv_w, conv_b, W_bc, b_bc, log_decay, W_out, b_out):
        import jax, jax.numpy as jnp
        import numpy as np
        from jax import lax
        D_MODEL, D_CONV, EXPAND = (256, 4, 2)
        D_INNER = D_MODEL * EXPAND
        B, N = (4, 512)
        Bsz, Nlen, _ = x.shape
        d_inner = conv_w.shape[0]
        d_conv = conv_w.shape[-1]
        ug = x @ W_in + b_in
        u, gate = jnp.split(ug, 2, axis=-1)
        u_t = jnp.transpose(u, (0, 2, 1))
        u_conv = lax.conv_general_dilated(u_t, conv_w, window_strides=(1,), padding=[(d_conv - 1, 0)], dimension_numbers=('NCH', 'OIH', 'NCH'), feature_group_count=d_inner)
        u_conv = u_conv + conv_b[None, :, None]
        u_conv = jnp.transpose(u_conv, (0, 2, 1))
        u_conv = jax.nn.silu(u_conv)
        bc = u_conv @ W_bc + b_bc
        b, c = jnp.split(bc, 2, axis=-1)
        a = jnp.exp(-jax.nn.softplus(log_decay)).astype(x.dtype)

        def step(state, bc_t):
            b_t, c_t = bc_t
            state = state * a + b_t
            return (state, state * c_t)
        xs = (jnp.moveaxis(b, 1, 0), jnp.moveaxis(c, 1, 0))
        init = jnp.zeros((Bsz, d_inner), x.dtype)
        _, ys = lax.scan(step, init, xs)
        y = jnp.moveaxis(ys, 0, 1)
        y = y * jax.nn.sigmoid(gate)
        return y @ W_out + b_out

    def _L0_ffn_ref(x, gate_w, gate_b, sw1, sb1, sw2, sb2, rw1, rb1, rw2, rb2):
        import jax, jax.numpy as jnp
        import numpy as np
        B, S, D, F, O = (4, 512, 256, 1024, 256)
        E, NS, K = (4, 2, 2)
        weights = jax.nn.softmax(x @ gate_w + gate_b, axis=-1)
        topk_w, topk_i = jax.lax.top_k(weights, K)
        sh = jax.nn.relu(jnp.einsum('bsd,ndf->bsnf', x, sw1) + sb1)
        shared = (jnp.einsum('bsnf,nfo->bsno', sh, sw2) + sb2).sum(axis=2) / NS
        rh = jax.nn.relu(jnp.einsum('bsd,edf->bsef', x, rw1) + rb1)
        eo = jnp.einsum('bsef,efo->bseo', rh, rw2) + rb2
        gathered = jnp.take_along_axis(eo, topk_i[..., None], axis=2)
        routed = (gathered * topk_w[..., None]).sum(axis=2)
        return shared + routed

    def _L1_attn_ref(x, Wq, Wk, Wv, Wo, b_o, rel_k_emb, rel_v_emb):
        import jax, jax.numpy as jnp
        import numpy as np
        import math
        D_MODEL = 256
        N_HEADS = 16
        D_K = D_MODEL // N_HEADS
        MAX_REL = 32
        B, S, D = x.shape
        H, dk = (N_HEADS, D_K)
        inv_sqrt_dk = 1.0 / math.sqrt(dk)
        Q = (x @ Wq.T).reshape(B, S, H, dk)
        K = (x @ Wk.T).reshape(B, S, H, dk)
        V = (x @ Wv.T).reshape(B, S, H, dk)
        pos = jnp.arange(S)
        rel_idx = jnp.clip(pos[None, :] - pos[:, None], -MAX_REL, MAX_REL) + MAX_REL
        rel_k = rel_k_emb[rel_idx]
        rel_v = rel_v_emb[rel_idx]
        scores = jnp.einsum('bihd,bjhd->bhij', Q, K) * inv_sqrt_dk
        scores = scores + jnp.einsum('bihd,ijd->bhij', Q, rel_k) * inv_sqrt_dk
        attn = jax.nn.softmax(scores, axis=-1)
        ctx = jnp.einsum('bhij,bjhd->bihd', attn, V)
        ctx = ctx + jnp.einsum('bhij,ijd->bihd', attn, rel_v)
        ctx = ctx.reshape(B, S, D)
        out = ctx @ Wo.T + b_o
        return out

    def _L1_ffn_ref(x, router_w, w1, b1, w2, b2):
        import jax, jax.numpy as jnp
        import numpy as np
        NUM_EXPERTS = 8
        TOP_K = 2
        B, S, H = x.shape
        xt = x.reshape(-1, H)
        router_logits = jnp.matmul(xt, router_w)
        router_probs = jax.nn.softmax(router_logits, axis=-1)
        top_k_probs, top_k_indices = jax.lax.top_k(router_probs, TOP_K)
        top_k_probs = top_k_probs / jnp.sum(top_k_probs, axis=-1, keepdims=True)
        one_hot = jax.nn.one_hot(top_k_indices, NUM_EXPERTS, dtype=xt.dtype)
        combine = jnp.einsum('tk,tke->te', top_k_probs, one_hot)
        expert_out = jnp.matmul(jax.nn.gelu(jnp.matmul(xt, w1) + b1), w2) + b2
        out = expert_out * jnp.sum(combine, axis=-1, keepdims=True)
        return out.reshape(B, S, H)
    h = _L0_tok_ref(x, L0_tok_Wqkv, L0_tok_Wproj)
    h = h + _L0_attn_ref(_layernorm(h, axis=-1), L0_attn_W_in, L0_attn_b_in, L0_attn_conv_w, L0_attn_conv_b, L0_attn_W_bc, L0_attn_b_bc, L0_attn_log_decay, L0_attn_W_out, L0_attn_b_out)
    h = h + _L0_ffn_ref(_layernorm(h, axis=-1), L0_ffn_gate_w, L0_ffn_gate_b, L0_ffn_sw1, L0_ffn_sb1, L0_ffn_sw2, L0_ffn_sb2, L0_ffn_rw1, L0_ffn_rb1, L0_ffn_rw2, L0_ffn_rb2)
    h = h + _L1_attn_ref(_layernorm(h, axis=-1), L1_attn_Wq, L1_attn_Wk, L1_attn_Wv, L1_attn_Wo, L1_attn_b_o, L1_attn_rel_k_emb, L1_attn_rel_v_emb)
    h = h + _L1_ffn_ref(_layernorm(h, axis=-1), L1_ffn_router_w, L1_ffn_w1, L1_ffn_b1, L1_ffn_w2, L1_ffn_b2)
    return h

_drawn_inputs = setup_inputs


def setup_inputs(seed=0):
    import zlib

    import numpy as np

    out = dict(_drawn_inputs(seed))
    spreads = {'L0_attn_b_in': (0.0, 0.558),
     'L0_attn_conv_b': (0.0, 0.289),
     'L0_attn_b_bc': (0.0, 0.1),
     'L0_attn_log_decay': (0.0, 0.8),
     'L0_attn_b_out': (0.0, 0.1),
     'L0_ffn_gate_b': (0.0, 0.1),
     'L0_ffn_sb1': (0.0, 0.1),
     'L0_ffn_sb2': (0.0, 0.1),
     'L0_ffn_rb1': (0.0, 0.1),
     'L0_ffn_rb2': (0.0, 0.1),
     'L1_attn_b_o': (0.0, 0.1),
     'L1_ffn_b1': (0.0, 0.1),
     'L1_ffn_b2': (0.0, 0.1)}
    factors = {'L1_attn_Wq': 3.432,
     'L1_attn_Wk': 3.391,
     'L1_attn_rel_k_emb': 8.0,
     'L1_attn_rel_v_emb': 4.344,
     'L1_ffn_router_w': 8.0}
    for name, (base, spread) in spreads.items():
        noise = np.random.default_rng([zlib.crc32(name.encode()), seed]).standard_normal(out[name].shape)
        drawn = base * np.exp(spread * noise) if base else spread * noise
        out[name] = jnp.asarray(drawn.astype(out[name].dtype))
    for name, factor in factors.items():
        out[name] = (out[name] * factor).astype(out[name].dtype)
    return out
```

```python
import concourse.bass as bass
from concourse import mybir
from contextlib import ExitStack

F32 = mybir.dt.float32
F32R = mybir.dt.float32r
ALU = mybir.AluOpType
ACT = mybir.ActivationFunctionType
AX = mybir.AxisListType

P = 128
B, S, D = 32, 192, 256
RAW_S = 256
H, DH = 16, 16
KT = D // P
GB = 2
GT = GB * S
TPG = GT // P
NG = B // GB
NT = B * S // P
HALF = 96
NJ = S // HALF
PAIRS = H // 2
M3 = S // 3
LN_EPS = 1e-5
DI = 512
IT = DI // P
DC = 4
FF = 1024
FT = FF // P
SHARED, ROUTED = 2, 4
CLASSES = 8
MAXREL = 32
QB = 64
WIN = QB + 2 * MAXREL
BAND = QB + 2 * MAXREL - 1
ROW = S


def mm3(pe, out, lhs, rhs, start=True, stop=True, skip=False):
    n = len(lhs)
    for k in range(n):
        (lh, ll), (rh, rl) = lhs[k], rhs[k]
        pe.matmul(out, lh, rh, start=start and k == 0, stop=False, skip_group_check=skip)
        pe.matmul(out, lh, rl, start=False, stop=False, skip_group_check=skip)
        last = pe.matmul(out, ll, rh, start=False, stop=stop and k == n - 1, skip_group_check=skip)
    return last


class Mem:

    def __init__(self, nc, ctx, tag):
        self.nc, self.ctx, self.tag = nc, ctx, tag

    def sb(self, name, shape, dt=F32):
        return self.ctx.enter_context(self.nc.sbuf_tensor(f"{self.tag}_{name}", shape, dt))

    def ps(self, name, shape):
        return self.ctx.enter_context(self.nc.psum_tensor(f"{self.tag}_{name}", shape, F32))

    def sem(self, name):
        return self.ctx.enter_context(self.nc.semaphore(f"{self.tag}_{name}"))


class Ring:

    def __init__(self, done, act, dve, readers, depth):
        self.done, self.sems, self.readers, self.depth = done, {"A": act, "D": dve}, readers, depth
        self.n = len(readers)

    def credit(self, eng, letter, more=0):
        eng.sem_inc(self.sems[letter], self.depth + more)

    def count(self, letter, first, last):
        return last - first if letter == "P" else sum(letter in r for r in self.readers[first:last])

    def upto(self, letter, use):
        if use >= 0:
            return sum(letter in r for r in self.readers[:use + 1])
        return -sum(letter in r for r in self.readers[self.n + use + 1:])

    def filled(self, eng, g, use):
        eng.wait_ge(self.done, g * self.n + use + 1 + self.n)

    def copied_by(self, eng, g, use, letter):
        per = sum(letter in r for r in self.readers)
        eng.wait_ge(self.sems[letter], g * per + self.upto(letter, use) + self.depth)

    def copied(self, eng, g, use):
        for letter in self.readers[use]:
            self.copied_by(eng, g, use, letter)

    def free(self, eng, g, use):
        self.copied(eng, g, use - self.depth)


class Norm:

    def __init__(self, mem, Hs):
        self.Hs = Hs
        self.stats = mem.sb("stats", [P, NT, 6])
        self.meanvar = mem.sb("meanvar", [P, NT, 2])
        self.vareps = mem.sb("vareps", [P, NT])
        self.std = mem.sb("std", [P, NT])
        self.y0 = mem.sb("y0", [P, NT])
        self.newton = mem.sb("newton", [P, NT])
        self.rstd = mem.sb("rstd", [P, NT])
        self.chain = mem.sem("norm_chain")
        self.root = mem.sem("norm_root")

    def vector(self, dve):
        for t in range(NT):
            last = dve.bn_stats(self.stats[:, t, :], self.Hs[:, t, :])
        last.then_inc(self.chain, 1)
        dve.wait_ge(self.chain, 1)
        for t in range(NT):
            last = dve.bn_aggr(self.meanvar[:, t, :], self.stats[:, t, :])
        last.then_inc(self.chain, 1)
        dve.wait_ge(self.chain, 2)
        dve.tensor_scalar(self.vareps[:, :], self.meanvar[:, :, 1], LN_EPS, None, ALU.add).then_inc(self.chain, 1)
        dve.wait_ge(self.root, 1)
        dve.reciprocal(self.y0[:, :], self.std[:, :]).then_inc(self.chain, 1)
        dve.wait_ge(self.chain, 4)
        dve.tensor_tensor(self.newton[:, :], self.y0[:, :], self.y0[:, :], ALU.mult).then_inc(self.chain, 1)
        dve.wait_ge(self.chain, 5)
        dve.tensor_tensor(self.newton[:, :], self.newton[:, :], self.vareps[:, :], ALU.mult).then_inc(self.chain, 1)
        dve.wait_ge(self.chain, 6)
        dve.tensor_scalar(self.newton[:, :], self.newton[:, :], -0.5, 1.5, ALU.mult, ALU.add).then_inc(self.chain, 1)
        dve.wait_ge(self.chain, 7)
        dve.tensor_tensor(self.rstd[:, :], self.y0[:, :], self.newton[:, :], ALU.mult).then_inc(self.chain, 1)
        dve.wait_ge(self.chain, 8)

    def scalar(self, act):
        act.wait_ge(self.chain, 3)
        act.activation(self.std[:, :], self.vareps[:, :], ACT.Sqrt).then_inc(self.root, 1)

    def apply(self, dve, out, n):
        one = bass.ds(n, 1)
        return dve.tensor_scalar(out, self.Hs[:, one, :].rearrange("p t d -> p (t d)"),
                                 self.meanvar[:, one, 0], self.rstd[:, one], ALU.subtract, ALU.mult)



PARTS = {0: [(0, P, 0)], 1: [(0, QB, 0), (QB, QB, 1)], 2: [(0, P, 1)]}
THIRD = {0: (0, 1), 1: (2, 0), 2: (1, 2)}


def window(third):
    first = QB * third - MAXREL
    return max(first, 0), min(first + WIN, S), max(-first, 0)


def attention(nc, Hs, dram, rel):
    ctx = ExitStack()
    with ctx:
        mem = Mem(nc, ctx, "a1" if rel else "a0")
        sb, sem = mem.sb, mem.sem
        w_raw = sb("w_raw", [P, KT, 4 * D])
        w_hi = sb("w_hi", [P, KT, 4 * D], F32R)
        w_lo = sb("w_lo", [P, KT, 4 * D], F32R)
        ident = sb("ident", [P, P])
        masks = sb("masks", [P, 2])
        if rel:
            norm = Norm(mem, Hs)
            xn = sb("xn", [P, TPG, D])
            x_hi = sb("x_hi", [P, KT, GT], F32R)
            x_lo = sb("x_lo", [P, KT, GT], F32R)
            relk = sb("relk", [P, 2 * MAXREL + 1])
            relkd = sb("relkd", [P, PAIRS // KT, 2 * MAXREL])
            relv = sb("relv", [P, DH])
            relv0 = sb("relv0", [P, DH])
            relvd = sb("relvd", [P, DH])
            rband = sb("rband", [P, 2, H, BAND])
            swin = sb("swin", [P, 2, H, WIN])
            punsk = sb("punsk", [P, H, BAND + 1])
            puT = sb("puT", [P, 2, 4, P])
            ctxraw = sb("ctxraw", [P, 2, D])
            bout = sb("bout", [P, D])
            outb = sb("outb", [P, D])
        else:
            xg = sb("xg", [P, 2, KT, 4, P])
            x_hi = sb("x_hi", [P, KT, 4, P], F32R)
            x_lo = sb("x_lo", [P, KT, 4, P], F32R)
            vT = sb("vT", [P, KT, GT])
        q_even = sb("q_even", [P, KT, GT])
        q_odd = sb("q_odd", [P, KT, GT])
        kT = sb("kT", [P, KT, GT])
        v = sb("v", [HALF, GB, NJ, D])
        probs = sb("probs", [P, 2, H, S])
        negmax = sb("negmax", [P, 4, 2])
        sums = sb("sums", [P, 2, H])
        rinv = sb("rinv", [P, 2, H])
        pT = sb("pT", [HALF, 2, 2, NJ, P])
        ctxn = sb("ctxn", [P, D])
        c_hi = sb("c_hi", [P, KT, P], F32R)
        c_lo = sb("c_lo", [P, KT, P], F32R)
        NSB = 3
        scores = mem.ps("scores", [P, NSB, 512])
        trans = mem.ps("trans", [P, 2, 512])
        ctxp = mem.ps("ctxp", [P, 512])
        proj = mem.ps("proj", [P, 2, 512])
        STEPS = TPG * PAIRS
        QUADS = H // 4

        if rel:
            puses = [("x", 0, "AD"), ("x", 1, "AD"), ("q", 0, "A"), ("q", 1, "D"), ("k", 0, "A"), ("k", 1, "D"),
                     ("v", 0, "A"), ("v", 1, "D"), ("r", (0, 0), "A"), ("r", (0, 1), "A"),
                     ("r", (1, 0), "A"), ("r", (1, 1), "A"), ("r", (2, 0), "A"), ("r", (2, 1), "A")]
            puses += [(name, t, r) for t in range(TPG) for name, r in (("rv", "D"), ("c", "AD"), ("o", "D"))]
            puses += [("pad", 0, "")]
        else:
            puses = [("q", 0, "A"), ("q", 1, "D"), ("k", 0, "A"), ("k", 1, "D"), ("vT", 0, "A"), ("vT", 1, "D"),
                     ("v", 0, "A"), ("v", 1, "D")]
            puses += [(name, t, r) for t in range(TPG) for name, r in (("c", "AD"), ("o", "A"))]
        PU = {(name, arg): n for n, (name, arg, _) in enumerate(puses)}
        tuses = []
        for s in range(STEPS):
            t, p = divmod(s, PAIRS)
            tuses.append(("s", s, "A" if rel and s % 2 else "D"))
            if rel and t and p >= QUADS:
                tuses.append(("u", (t - 1, p - QUADS), "A"))
        if rel:
            tuses += [("u", (TPG - 1, q), "A") for q in range(QUADS)]
        TU = {(name, arg): n for n, (name, arg, _) in enumerate(tuses)}
        proj_ring = Ring(sem("proj_done"), sem("proj_act"), sem("proj_dve"), [r for *_, r in puses], 2)
        trans_ring = Ring(sem("trans_done"), sem("trans_act"), sem("trans_dve"), [r for *_, r in tuses], 2)

        w_in = sem("w_in")
        w_hi_ready = sem("w_hi_ready")
        w_split = sem("w_split")
        x_in = [sem("x_in_even"), sem("x_in_odd")]
        x_split = sem("x_split")
        xn_ready = sem("xn_ready")
        s_done = sem("s_done")
        rel_added = sem("rel_added")
        max_ready = sem("max_ready")
        p_ready = sem("p_ready")
        v_used = sem("v_used")
        ctx_out = sem("ctx_out")
        rc_ready = sem("rc_ready")
        cn_chain = sem("cn_chain")
        cn_ready = sem("cn_ready")
        out_added = sem("out_added")
        sw_in = sem("sw_in")
        r_out = sem("r_out")
        pw_out = sem("pw_out")
        pu_in = sem("pu_in")
        far_ready = sem("far_ready")
        rel_done = sem("rel_done")
        zeroed = sem("zeroed")
        table_zeroed = sem("table_zeroed")
        z_out = sem("z_out")
        P_CREDIT = 2 * NSB

        loads = [(w_raw[:, :, :], dram["w_rel" if rel else "w_tok"]), (ident[:, :], dram["ident"]),
                 (masks[:, :], dram["masks_rel" if rel else "masks_tok"])]
        if rel:
            loads += [(relk[DH * h:DH * (h + 1), :], dram["rel_kT"]) for h in range(P // DH)]
            loads += [(relv[0:2 * MAXREL, :], dram["rel_v"][1:2 * MAXREL + 1, :]),
                      (relv[2 * MAXREL:P, :],
                       dram["rel_v"][2 * MAXREL:2 * MAXREL + 1, :].broadcast_to([P - 2 * MAXREL, DH])),
                      (relv0[:, :], dram["rel_v"][0:1, :].broadcast_to([P, DH])),
                      (bout[:, :], dram["b_o"].broadcast_to([P, D]))]
        W_ALL = 16 * len(loads)
        SPLITS = 3 if rel else 1

        def w(col, n, k):
            return (w_hi[:, k, col:col + n], w_lo[:, k, col:col + n])

        def slot(half, t):
            return (half * TPG + t) % 2

        def pair_rows(p):
            f, quad = divmod(p, PAIRS // KT)
            return f, slice(32 * quad, 32 * quad + 32)

        def bank_order(ap):
            return ap[:, 0:GT] if rel else ap[:, 0:GT].rearrange("p (r b m) -> p r b m", r=3, b=GB)

        def token_order(ap):
            return ap if rel else ap.rearrange("p (b m r) -> p r b m", r=3, b=GB)

        def key_order(ap):
            return ap if rel else ap.rearrange("p (b r m) -> p r b m", r=3, b=GB)

        block = ctx.enter_context(nc.Block())

        @block.sync
        def _(sp):
            for dst, src in loads:
                sp.dma_start(dst, src).then_inc(w_in, 16)
            if not rel:
                for g in range(2):
                    sp.dma_start(xg[:, g, :, :, :], dram["x"][g, :, :, :, :]).then_inc(x_in[g], 16)
                with sp.Fori(0, NG // 2 - 1) as gg:
                    for half in range(2):
                        g = gg * 2 + half
                        sp.wait_ge(x_split, 2 * g + 2)
                        sp.dma_start(xg[:, half, :, :, :],
                                     dram["x"][bass.ds(g + 2, 1), :, :, :, :].rearrange("g p k o m -> (g p) k o m")
                                     ).then_inc(x_in[half], 16)
                return
            sp.wait_ge(zeroed, 1)
            for buf in (dram["skew_s"], dram["skew_p"]):
                for t in range(TPG):
                    sp.dma_start(buf[t, :, :, :], probs[:, 0, :, :]).then_inc(z_out, 16)
            sp.wait_ge(z_out, 16 * 2 * TPG)
            sp.sem_inc(r_out, 32)
            sp.sem_inc(pw_out, 64)

            def skew_scores(g, half, t):
                n = g * TPG + t
                proj_ring.copied(sp, g, PU["r", (t, 1)])
                sp.wait_ge(rel_added, PAIRS * n + PAIRS)
                sp.dma_start(dram["skew_s"][t, :, :, QB:QB + BAND], rband[:, slot(half, t), :, :]
                             ).then_inc(r_out, 16)
                sp.wait_ge(r_out, 16 * n + 16 + 32)
                for part in range(2):
                    src = bass.AP(dram["skew_s"].tensor, (t * P + part * QB) * H * ROW + QB - 1,
                                  [[H * ROW - 1, QB], [ROW, H], [1, WIN]])
                    sp.dma_start(swin[part * QB:(part + 1) * QB, slot(half, t), :, :], src).then_inc(sw_in, 16)

            def unskew_probs(g, half, t):
                n = g * TPG + t
                sp.wait_ge(p_ready, H * n + H + P_CREDIT)
                for part in range(2):
                    k0, k1, x0 = window(THIRD[t][part])
                    rows = slice(part * QB, (part + 1) * QB)
                    sp.dma_start(dram["skew_p"][t, rows, :, x0:x0 + k1 - k0],
                                 probs[rows, slot(half, t), :, k0:k1]).then_inc(pw_out, 16)
                sp.wait_ge(pw_out, 32 * n + 32 + 64)
                sp.wait_ge(rel_done, QUADS * n + QUADS)
                for part in range(2):
                    src = bass.AP(dram["skew_p"].tensor, (t * P + part * QB) * H * ROW + 1,
                                  [[H * ROW + 1, QB], [ROW, H], [1, BAND]])
                    sp.dma_start(punsk[part * QB:(part + 1) * QB, :, 0:BAND], src).then_inc(pu_in, 16)

            with sp.Fori(0, NG // 2) as gg:
                for half in range(2):
                    g = gg * 2 + half
                    skew_scores(g, half, 0)
                    skew_scores(g, half, 1)
                    unskew_probs(g, half, 0)
                    skew_scores(g, half, 2)
                    unskew_probs(g, half, 1)
                    unskew_probs(g, half, 2)

        @block.tensor
        def _(pe):
            def project(g):
                if rel:
                    for k in range(KT):
                        use = PU["x", k]
                        proj_ring.free(pe, g, use)
                        if k == 0:
                            pe.wait_ge(xn_ready, TPG * g + TPG)
                        for t in range(TPG):
                            last = pe.transpose(proj[:, use % 2, t * P:(t + 1) * P], xn[:, t, k * P:(k + 1) * P],
                                                ident[:, :])
                        last.then_inc(proj_ring.done, 1)
                    proj_ring.copied(pe, g, PU["x", 1])
                else:
                    pe.wait_ge(x_split, 2 * g + 2)
                for n, name in enumerate(("q", "k", "v" if rel else "vT")):
                    for f in range(KT):
                        use = PU[name, f]
                        proj_ring.free(pe, g, use)
                        out = proj[:, use % 2, :]
                        if not rel:
                            for r in range(3):
                                o, j = divmod(4 * r + n, 3)
                                last = mm3(pe, out[:, r * P:(r + 1) * P],
                                           [w(j * D + f * P, P, k) for k in range(KT)],
                                           [(x_hi[:, k, o, :], x_lo[:, k, o, :]) for k in range(KT)])
                        elif name != "v":
                            last = mm3(pe, out[:, 0:GT], [w(n * D + f * P, P, k) for k in range(KT)],
                                       [(x_hi[:, k, :], x_lo[:, k, :]) for k in range(KT)])
                        else:
                            for j in range(NJ):
                                tok = slice(f * S + j * HALF, f * S + (j + 1) * HALF)
                                last = mm3(pe, out[0:HALF, j * D:(j + 1) * D],
                                           [(x_hi[:, k, tok], x_lo[:, k, tok]) for k in range(KT)],
                                           [w(n * D, D, k) for k in range(KT)])
                        last.then_inc(proj_ring.done, 1)
                if not rel:
                    proj_ring.copied(pe, g, PU["vT", 0])
                    proj_ring.copied(pe, g, PU["vT", 1])
                    for b in range(GB):
                        use = PU["v", b]
                        proj_ring.free(pe, g, use)
                        for j in range(NJ):
                            for k in range(KT):
                                c = (j * KT + k) * P
                                last = pe.transpose(proj[0:HALF, use % 2, c:c + P],
                                                    vT[:, k, b * S + j * HALF:b * S + (j + 1) * HALF], ident[:, :])
                        last.then_inc(proj_ring.done, 1)
                proj_ring.copied(pe, g, PU["v", 0])
                proj_ring.copied(pe, g, PU["v", 1])

            def score(g, s):
                t, p = divmod(s, PAIRS)
                f, rows = pair_rows(p)
                pe.wait_ge(p_ready, 2 * (g * STEPS + s + 1 - NSB) + P_CREDIT)
                for h, q in enumerate((q_even, q_odd)):
                    for p0, n, b in PARTS[t]:
                        last = pe.matmul(scores[p0:p0 + n, s % NSB, h * S:(h + 1) * S],
                                         q[rows, f, t * P + p0:t * P + p0 + n],
                                         kT[rows, f, b * S:(b + 1) * S], start=True, stop=True)
                last.then_inc(s_done, 1)

            def turn(g, half, s):
                t, p = divmod(s, PAIRS)
                use = TU["s", s]
                trans_ring.free(pe, g, use)
                pe.wait_ge(p_ready, 2 * (g * STEPS + s + 1) + P_CREDIT)
                for h in range(2):
                    for j in range(NJ):
                        c = (h * NJ + j) * P
                        last = pe.transpose(trans[0:HALF, use % 2, c:c + P],
                                            probs[:, slot(half, t), 2 * p + h, j * HALF:(j + 1) * HALF],
                                            ident[:, :])
                last.then_inc(trans_ring.done, 1)

            def values(g, s):
                t, p = divmod(s, PAIRS)
                if p == 0:
                    pe.wait_ge(ctx_out if rel else cn_ready, g * TPG + t + 1)
                trans_ring.copied(pe, g, TU["s", s])
                for h in range(2):
                    c = (2 * p + h) * DH
                    for p0, n, b in PARTS[t]:
                        for j in range(NJ):
                            last = pe.matmul(ctxp[p0:p0 + n, c:c + DH], pT[:, s % 2, h, j, p0:p0 + n],
                                             v[:, b, j, c:c + DH], start=(j == 0), stop=(j == NJ - 1))
                last.then_inc(v_used, 1)

            def relscore(g, t):
                for part in range(2):
                    use = PU["r", (t, part)]
                    proj_ring.free(pe, g, use)
                    for odd, q in enumerate((q_even, q_odd)):
                        c = odd * (PAIRS // KT) * 2 * MAXREL
                        last = pe.matmul(proj[:, use % 2, c:c + (PAIRS // KT) * 2 * MAXREL],
                                         q[:, part, t * P:(t + 1) * P],
                                         relkd[:, :, :].rearrange("p a r -> p (a r)"), start=True, stop=True)
                    last.then_inc(proj_ring.done, 1)

            def relturn(g, t, quad):
                use = TU["u", (t, quad)]
                trans_ring.free(pe, g, use)
                if quad == 0:
                    pe.wait_ge(pu_in, 32 * (g * TPG + t) + 32)
                    pe.wait_ge(far_ready, g * TPG + t + 1 + 2)
                for i in range(4):
                    last = pe.transpose(trans[:, use % 2, i * P:(i + 1) * P], punsk[:, 4 * quad + i, :],
                                        ident[:, :])
                last.then_inc(trans_ring.done, 1)

            def relvalues(g, t, quad):
                use = PU["rv", t]
                if quad == 0:
                    proj_ring.free(pe, g, use)
                trans_ring.copied(pe, g, TU["u", (t, quad)])
                for i in range(4):
                    c = (4 * quad + i) * DH
                    last = pe.matmul(proj[:, use % 2, c:c + DH], puT[:, quad % 2, i, :], relvd[:, :],
                                     start=True, stop=True)
                    if quad == QUADS - 1 and i == 2:
                        last.then_inc(proj_ring.done, 1)
                last.then_inc(rel_done, 1)

            def turn_ctx(g, t):
                use = PU["c", t]
                proj_ring.free(pe, g, use)
                pe.wait_ge(cn_ready, g * TPG + t + 2)
                for k in range(KT):
                    last = pe.transpose(proj[:, use % 2, k * P:(k + 1) * P], ctxn[:, k * P:(k + 1) * P], ident[:, :])
                last.then_inc(proj_ring.done, 1)

            def project_out(g, t):
                use = PU["o", t]
                proj_ring.free(pe, g, use)
                proj_ring.copied(pe, g, PU["c", t])
                mm3(pe, proj[:, use % 2, 0:D], [(c_hi[:, k, :], c_lo[:, k, :]) for k in range(KT)],
                    [w(3 * D, D, k) for k in range(KT)]).then_inc(proj_ring.done, 2 if ("pad", 0) in PU and t == 2 else 1)

            pe.sem_inc(proj_ring.done, proj_ring.n)
            pe.sem_inc(trans_ring.done, trans_ring.n)
            if rel:
                pe.sem_inc(rel_done, QUADS)
            pe.wait_ge(w_in, W_ALL)
            pe.wait_ge(w_split, SPLITS)
            with pe.Fori(0, NG // 2) as gg:
                for half in range(2):
                    g = gg * 2 + half
                    project(g)
                    if rel:
                        relscore(g, 0)
                        relscore(g, 1)
                    score(g, 0)
                    score(g, 1)
                    for s in range(STEPS):
                        t, p = divmod(s, PAIRS)
                        if s + 2 < STEPS:
                            score(g, s + 2)
                        turn(g, half, s)
                        if s >= 1:
                            values(g, s - 1)
                        if rel and t:
                            if p >= QUADS:
                                relturn(g, t - 1, p - QUADS)
                            if p > QUADS:
                                relvalues(g, t - 1, p - QUADS - 1)
                        if rel and (t, p) == (1, 1):
                            relscore(g, 2)
                        if rel and (t, p) == (2, 0):
                            relvalues(g, 0, QUADS - 1)
                        if t and not rel or t == 2:
                            if p == 2:
                                turn_ctx(g, t - 2 if rel else t - 1)
                            if p == 3:
                                project_out(g, t - 2 if rel else t - 1)
                    values(g, STEPS - 1)
                    if rel:
                        relvalues(g, 1, QUADS - 1)
                        turn_ctx(g, 1)
                        project_out(g, 1)
                        for quad in range(QUADS):
                            relturn(g, 2, quad)
                            relvalues(g, 2, quad)
                    turn_ctx(g, 2)
                    project_out(g, 2)

        @block.scalar
        def _(act):
            proj_ring.credit(act, "A")
            trans_ring.credit(act, "A")
            act.sem_inc(p_ready, P_CREDIT)
            act.wait_ge(w_in, W_ALL)
            act.activation(w_hi[:, :, :], w_raw[:, :, :], ACT.Identity).then_inc(w_hi_ready, 1)
            if rel:
                norm.scalar(act)

            def bank_of(name, arg):
                return proj[:, PU[name, arg] % 2, :]

            def copy(g, name, arg, out, src, scale=1.0):
                proj_ring.filled(act, g, PU[name, arg])
                act.activation(out, src, ACT.Identity, scale=scale).then_inc(proj_ring.sems["A"], 1)

            def read_band(g, half, t):
                n = g * TPG + t
                act.wait_ge(r_out, 16 * n + 16)
                act.wait_ge(rel_added, PAIRS * n + PAIRS)
                for part in range(2):
                    proj_ring.filled(act, g, PU["r", (t, part)])
                    bank = bank_of("r", (t, part)).rearrange("p (e a r) -> p a e r", e=2, r=2 * MAXREL)
                    band = rband[:, slot(half, t), part * H // 2:(part + 1) * H // 2, :].rearrange(
                        "p (a e) r -> p a e r", e=2)
                    act.activation(band[:, :, :, 0:2 * MAXREL], bank, ACT.Identity)
                    act.activation(band[:, :, :, 2 * MAXREL:BAND], bank[:, :, :, 2 * MAXREL - 1:2 * MAXREL].broadcast_to(
                        [P, PAIRS // KT, 2, BAND - 2 * MAXREL]), ACT.Identity).then_inc(proj_ring.sems["A"], 1)

            def exponentials(g, half, s):
                t, p = divmod(s, PAIRS)
                if rel and p == 0:
                    act.wait_ge(pw_out, 32 * (g * TPG + t) + 32)
                    act.wait_ge(far_ready, g * TPG + t + 1)
                act.wait_ge(max_ready, g * STEPS + s + 1)
                for h in range(2):
                    act.activation(probs[:, slot(half, t), 2 * p + h, :], scores[:, s % NSB, h * S:(h + 1) * S],
                                   ACT.Exp, bias=negmax[:, s % 4, h:h + 1],
                                   accum_out=sums[:, slot(half, t), 2 * p + h:2 * p + h + 1]).then_inc(p_ready, 1)

            def copy_turned(g, s):
                use = TU["s", s]
                trans_ring.filled(act, g, use)
                act.activation(pT[:, s % 2, :, :, :].rearrange("k h j q -> k (h j q)"), trans[0:HALF, use % 2, :],
                               ACT.Identity).then_inc(trans_ring.sems["A"], 1)

            def copy_relturned(g, t, quad):
                use = TU["u", (t, quad)]
                trans_ring.filled(act, g, use)
                act.activation(puT[:, quad % 2, :, :].rearrange("r h q -> r (h q)"), trans[:, use % 2, :],
                               ACT.Identity).then_inc(trans_ring.sems["A"], 1)

            def split_ctx(g, t):
                copy(g, "c", t, c_hi[:, :, :].rearrange("p k q -> p (k q)"), bank_of("c", t)[:, 0:D])

            def store_out(g, t):
                copy(g, "o", t, Hs[:, bass.ds(g * TPG + t, 1), :].rearrange("p t d -> p (t d)"),
                     bank_of("o", t)[:, 0:D])

            with act.Fori(0, NG // 2) as gg:
                for half in range(2):
                    g = gg * 2 + half
                    if rel:
                        for k in range(KT):
                            copy(g, "x", k, x_hi[:, k, :], bank_of("x", k)[:, 0:GT])
                    else:
                        act.wait_ge(x_in[half], 16 * gg + 16)
                        proj_ring.filled(act, g, PU["vT", 1] - proj_ring.n)
                        act.activation(x_hi[:, :, :, :], xg[:, half, :, :, :], ACT.Identity).then_inc(x_split, 1)
                    proj_ring.filled(act, g, PU["q", 0])
                    act.activation(token_order(q_even[:, 0, :]), bank_order(bank_of("q", 0)), ACT.Identity,
                                   scale=masks[:, 0:1])
                    copy(g, "q", 0, token_order(q_odd[:, 0, :]), bank_order(bank_of("q", 0)), masks[:, 1:2])
                    copy(g, "k", 0, key_order(kT[:, 0, :]), bank_order(bank_of("k", 0)))
                    if not rel:
                        copy(g, "vT", 0, key_order(vT[:, 0, :]), bank_order(bank_of("vT", 0)))
                    copy(g, "v", 0, v[:, 0, :, :].rearrange("k j d -> k (j d)"), bank_of("v", 0)[0:HALF, :])
                    if rel:
                        read_band(g, half, 0)
                        read_band(g, half, 1)
                    for s in range(STEPS + 1):
                        t, p = divmod(s, PAIRS)
                        if s < STEPS:
                            exponentials(g, half, s)
                        if rel and s and (s - 1) % 2:
                            copy_turned(g, s - 1)
                        if rel and s - 1 >= PAIRS and (s - 1) % PAIRS >= QUADS:
                            copy_relturned(g, (s - 1) // PAIRS - 1, (s - 1) % PAIRS - QUADS)
                        if rel and (t, p) == (1, 2):
                            read_band(g, half, 2)
                        if rel and t == 2 or not rel and t in (1, 2):
                            if p == 3:
                                split_ctx(g, t - 2 if rel else t - 1)
                            if p == 4 and not rel:
                                store_out(g, t - 1)
                    if rel:
                        split_ctx(g, 1)
                        for quad in range(QUADS):
                            copy_relturned(g, 2, quad)
                    split_ctx(g, 2)
                    if not rel:
                        store_out(g, 2)

        @block.vector
        def _(dve):
            proj_ring.credit(dve, "D")
            trans_ring.credit(dve, "D")
            dve.sem_inc(ctx_out, 1)
            dve.sem_inc(cn_ready, 1)
            dve.wait_ge(w_in, W_ALL)
            if rel:
                dve.sem_inc(rel_added, 2 * PAIRS)
                dve.sem_inc(far_ready, 2)
                dve.memset(probs[:, 0, :, :], 0.0).then_inc(zeroed, 1)
                dve.memset(relkd[:, :, :], 0.0).then_inc(table_zeroed, 1)
                dve.wait_ge(table_zeroed, 1)
                for a in range(PAIRS // KT):
                    rows = slice(32 * a, 32 * a + 32)
                    last = dve.tensor_scalar(relkd[rows, a, :], relk[rows, 1:2 * MAXREL + 1], relk[rows, 0:1], None,
                                             ALU.subtract)
                last.then_inc(w_split, 1)
                dve.tensor_tensor(relvd[:, :], relv[:, :], relv0[:, :], ALU.subtract).then_inc(w_split, 1)
                dve.wait_ge(z_out, 16 * 2 * TPG)
                norm.vector(dve)

            def bank_of(name, arg):
                return proj[:, PU[name, arg] % 2, :]

            def done(ins):
                ins.then_inc(proj_ring.sems["D"], 1)

            def copy(g, name, arg, out, src):
                proj_ring.filled(dve, g, PU[name, arg])
                done(dve.tensor_copy(out, src))

            def layernorm(g):
                for t in range(TPG):
                    norm.apply(dve, xn[:, t, :], g * TPG + t).then_inc(xn_ready, 1)

            def maxima(g, half, s):
                t, p = divmod(s, PAIRS)
                bank = scores[:, s % NSB, 0:2 * S].rearrange("q (h k) -> q h k", h=2)
                dve.wait_ge(s_done, g * STEPS + s + 1)
                if rel:
                    if p == 0:
                        dve.wait_ge(sw_in, 32 * (g * TPG + t) + 32)
                    for part in range(2):
                        k0, k1, x0 = window(THIRD[t][part])
                        rows = slice(part * QB, (part + 1) * QB)
                        last = dve.tensor_tensor(bank[rows, :, k0:k1],
                                                 swin[rows, slot(half, t), 2 * p:2 * p + 2, x0:x0 + k1 - k0],
                                                 bank[rows, :, k0:k1], ALU.add)
                        if k1 < S:
                            last = dve.tensor_tensor(bank[rows, :, k1:S],
                                                     rband[rows, slot(half, t), 2 * p:2 * p + 2, BAND - 1:BAND]
                                                     .broadcast_to([QB, 2, S - k1]), bank[rows, :, k1:S], ALU.add)
                    last.then_inc(rel_added, 1)
                    dve.wait_ge(rel_added, g * STEPS + s + 1 + 2 * PAIRS)
                dve.tensor_reduce(negmax[:, s % 4, :], bank, AX.X, ALU.max, negate=True).then_inc(max_ready, 1)

            def copy_turned(g, s):
                use = TU["s", s]
                trans_ring.filled(dve, g, use)
                dve.tensor_copy(pT[:, s % 2, :, :, :].rearrange("k h j q -> k (h j q)"), trans[0:HALF, use % 2, :]
                                ).then_inc(trans_ring.sems["D"], 1)

            def heads(ap):
                return ap.rearrange("p (h d) -> p h d", h=H)

            def reciprocals(g, half, t):
                n = g * TPG + t
                dve.wait_ge(p_ready, H * (n + 1) + P_CREDIT)
                dve.reciprocal(rinv[:, slot(half, t), :], sums[:, slot(half, t), :]).then_inc(rc_ready, 1)

            def per_head(half, t):
                return rinv[:, slot(half, t), :].unsqueeze(2).broadcast_to([P, H, DH])

            def far_sums(g, half, t):
                n = g * TPG + t
                dve.wait_ge(rel_done, QUADS * n + QUADS)
                for part in range(2):
                    _, k1, _ = window(THIRD[t][part])
                    rows = slice(part * QB, (part + 1) * QB)
                    if k1 < S:
                        last = dve.tensor_reduce(punsk[rows, :, BAND], probs[rows, slot(half, t), :, k1:S],
                                                  AX.X, ALU.add)
                    else:
                        last = dve.memset(punsk[rows, :, BAND], 0.0)
                last.then_inc(far_ready, 1)

            def read_ctx(g, half, t):
                n = g * TPG + t
                reciprocals(g, half, t)
                dve.wait_ge(v_used, PAIRS * (n + 1))
                if rel:
                    far_sums(g, half, t)
                    dve.tensor_copy(ctxraw[:, slot(half, t), :], ctxp[:, 0:D]).then_inc(ctx_out, 1)
                else:
                    dve.wait_ge(rc_ready, n + 1)
                    proj_ring.filled(dve, g, PU["c", t - 1] if t else PU["c", 2] - proj_ring.n)
                    dve.tensor_tensor(heads(ctxn[:, :]), heads(ctxp[:, 0:D]), per_head(half, t),
                                      ALU.mult).then_inc(cn_ready, 1)

            def combine(g, half, t):
                n = g * TPG + t
                dve.wait_ge(rel_done, QUADS * (n + 1) + QUADS)
                dve.wait_ge(ctx_out, n + 2)
                dve.wait_ge(rc_ready, n + 1)
                proj_ring.filled(dve, g, PU["c", t - 1] if t else PU["c", 2] - proj_ring.n)
                done(dve.tensor_tensor(ctxn[:, :], ctxraw[:, slot(half, t), :], bank_of("rv", t)[:, 0:D], ALU.add))
                proj_ring.copied(dve, g, PU["rv", t])
                dve.tensor_tensor(heads(ctxn[:, :]), heads(ctxn[:, :]), per_head(half, t),
                                  ALU.mult).then_inc(cn_chain, 1)
                dve.wait_ge(cn_chain, n + 1)
                dve.tensor_tensor(heads(ctxn[:, :]), heads(ctxn[:, :]),
                                  relv0[:, :].unsqueeze(1).broadcast_to([P, H, DH]), ALU.add).then_inc(cn_ready, 1)

            def split_ctx(g, t):
                proj_ring.copied_by(dve, g, PU["c", t], "A")
                done(dve.tensor_tensor(c_lo[:, :, :].rearrange("p k q -> p (k q)"), bank_of("c", t)[:, 0:D],
                                       c_hi[:, :, :].rearrange("p k q -> p (k q)").bitcast(F32), ALU.subtract))

            def out_bias(g, t):
                dve.wait_ge(out_added, g * TPG + t + 1)
                proj_ring.filled(dve, g, PU["o", t])
                done(dve.tensor_tensor(outb[:, :], bank_of("o", t)[:, 0:D], bout[:, :], ALU.add))

            with dve.Fori(0, NG // 2) as gg:
                for half in range(2):
                    g = gg * 2 + half
                    if rel:
                        layernorm(g)
                        for k in range(KT):
                            proj_ring.copied_by(dve, g, PU["x", k], "A")
                            done(dve.tensor_tensor(x_lo[:, k, :], bank_of("x", k)[:, 0:GT],
                                                   x_hi[:, k, :].bitcast(F32), ALU.subtract))
                    proj_ring.filled(dve, g, PU["q", 1])
                    dve.tensor_scalar(token_order(q_even[:, 1, :]), bank_order(bank_of("q", 1)), masks[:, 0:1],
                                      None, ALU.mult)
                    done(dve.tensor_scalar(token_order(q_odd[:, 1, :]), bank_order(bank_of("q", 1)), masks[:, 1:2],
                                           None, ALU.mult))
                    copy(g, "k", 1, key_order(kT[:, 1, :]), bank_order(bank_of("k", 1)))
                    if not rel:
                        copy(g, "vT", 1, key_order(vT[:, 1, :]), bank_order(bank_of("vT", 1)))
                    copy(g, "v", 1, v[:, 1, :, :].rearrange("k j d -> k (j d)"), bank_of("v", 1)[0:HALF, :])
                    for s in range(STEPS + 1):
                        t, p = divmod(s, PAIRS)
                        if s < STEPS:
                            maxima(g, half, s)
                        if s and not (rel and (s - 1) % 2):
                            copy_turned(g, s - 1)
                        if p == 1 and t:
                            read_ctx(g, half, t - 1)
                            if rel and t == 2:
                                combine(g, half, 0)
                        if rel and t == 2 or not rel and t in (1, 2):
                            if p == 3:
                                split_ctx(g, t - 2 if rel else t - 1)
                            if p == 4 and rel:
                                out_bias(g, 0)
                    read_ctx(g, half, 2)
                    if rel:
                        combine(g, half, 1)
                        split_ctx(g, 1)
                        out_bias(g, 1)
                        combine(g, half, 2)
                    split_ctx(g, 2)
                    if rel:
                        out_bias(g, 2)

        @block.gpsimd
        def _(pool):
            pool.wait_ge(w_in, W_ALL)
            pool.wait_ge(w_hi_ready, 1)
            pool.tensor_tensor(w_lo[:, :, :], w_raw[:, :, :], w_hi[:, :, :].bitcast(F32),
                               ALU.subtract).then_inc(w_split, 1)
            if rel:
                pool.sem_inc(out_added, 1)
                def add_out(g, t):
                    tile = Hs[:, bass.ds(g * TPG + t, 1), :].rearrange("p t d -> p (t d)")
                    proj_ring.copied_by(pool, g, PU["o", t], "D")
                    pool.tensor_tensor(tile, outb[:, :], tile, ALU.add).then_inc(out_added, 1)

                with pool.Fori(0, NG // 2) as gg:
                    for half in range(2):
                        g = gg * 2 + half
                        for t in range(TPG):
                            add_out(g, t)
            else:
                with pool.Fori(0, NG // 2) as gg:
                    for half in range(2):
                        g = gg * 2 + half
                        pool.wait_ge(x_in[half], 16 * gg + 16)
                        pool.wait_ge(x_split, 2 * g + 1)
                        pool.tensor_tensor(x_lo[:, :, :, :], xg[:, half, :, :, :],
                                           x_hi[:, :, :, :].bitcast(F32), ALU.subtract).then_inc(x_split, 1)



def recurrence(nc, Hs, dram):
    ctx = ExitStack()
    with ctx:
        mem = Mem(nc, ctx, "rc")
        sb, sem = mem.sb, mem.sem
        norm = Norm(mem, Hs)
        NW = KT * 2 * DI + IT * 2 * DI + IT * D
        w_raw = sb("w_raw", [P, NW])
        w_hi = sb("w_hi", [P, NW], F32R)
        w_lo = sb("w_lo", [P, NW], F32R)
        OUT0 = KT * 2 * DI + IT * 2 * DI
        ident = sb("ident", [P, P])
        b_in = sb("b_in", [P, 2 * IT])
        b_gate = sb("b_gate", [P, IT])
        conv_w = sb("conv_w", [P, IT, DC])
        conv_b = sb("conv_b", [P, IT])
        b_bc = sb("b_bc", [P, 2 * IT])
        log_decay = sb("log_decay", [P, IT])
        decay1 = sb("decay1", [P, IT])
        decay2 = sb("decay2", [P, IT])
        decay = sb("decay", [P, IT, GT])
        bout = sb("bout", [P, D])
        xn = sb("xn", [P, TPG, D])
        x_hi = sb("x_hi", [P, KT, GT], F32R)
        x_lo = sb("x_lo", [P, KT, GT], F32R)
        u = sb("u", [P, IT, GB, DC - 1 + S])
        conv = sb("conv", [P, IT, GT])
        uc_hi = sb("uc_hi", [P, IT, GT], F32R)
        uc_lo = sb("uc_lo", [P, IT, GT], F32R)
        gate = sb("gate", [P, IT, GT])
        bt = sb("bt", [P, 2, GT])
        state = sb("state", [P, 2, GT])
        y = w_raw[:, 0:IT * GT].rearrange("p (f t) -> p f t", f=IT)
        y_hi = sb("y_hi", [P, IT, GT], F32R)
        y_lo = sb("y_lo", [P, IT, GT], F32R)
        outb = sb("outb", [P, TPG, D])
        DEPTH = 8
        banks = mem.ps("banks", [P, DEPTH, 512])

        uses = [(name, f, r) for f in range(IT) for name, r in (("b", "A"), ("c", "D"))]
        A0 = len(uses)
        uses += [("x", k, "AD") for k in range(KT)] + [("u", f, "A") for f in range(IT)]
        uses += [("g", f, "A") for f in range(IT)]
        C0 = len(uses)
        uses += [("o", 0, "D"), ("o", 1, "D")]
        PADS = -len(uses) % DEPTH
        uses += [("pad", i, "") for i in range(PADS)]
        U = {(name, arg): n for n, (name, arg, _) in enumerate(uses)}
        ring = Ring(sem("done"), sem("act"), sem("dve"), [r for *_, r in uses], DEPTH)

        w_in = sem("w_in")
        scaled = sem("scaled")
        w_hi_ready = sem("w_hi_ready")
        w_split = sem("w_split")
        ready = sem("ready")
        tables = sem("tables")
        decay_act = sem("decay_act")
        xn_ready = sem("xn_ready")
        conv_chain = sem("conv_chain")
        uc_ready = sem("uc_ready")
        ucl_ready = sem("ucl_ready")
        state_ready = sem("state_ready")
        y1_ready = sem("y1_ready")
        y_ready = sem("y_ready")
        yh_ready = sem("yh_ready")
        yl_ready = sem("yl_ready")
        out_added = sem("out_added")

        loads = [(w_raw[:, :], dram["w_rc"]), (ident[:, :], dram["ident"]), (b_in[:, :], dram["rc_b_in"]),
                 (conv_w[:, :, :], dram["rc_conv_w"]), (conv_b[:, :], dram["rc_conv_b"]),
                 (b_bc[:, :], dram["rc_b_bc"]), (log_decay[:, :], dram["rc_log_decay"]),
                 (bout[:, :], dram["rc_b_out"].broadcast_to([P, D]))]
        W_ALL = 16 * len(loads)

        def part(base, k, width, col, n):
            c = base + k * width + col
            return (w_hi[:, c:c + n], w_lo[:, c:c + n])

        def w_in_at(k, col):
            return part(0, k, 2 * DI, col, P)

        def w_bc_at(k, col):
            return part(KT * 2 * DI, k, 2 * DI, col, P)

        def bank(name, arg):
            return banks[:, U[name, arg] % DEPTH, :]

        block = ctx.enter_context(nc.Block())

        @block.sync
        def _(sp):
            for dst, src in loads:
                sp.dma_start(dst, src).then_inc(w_in, 16)

        @block.tensor
        def _(pe):
            def stage_a(g, left_out=0):
                for k in range(KT):
                    ring.free(pe, g, U["x", k])
                    if k == 0:
                        pe.wait_ge(xn_ready, TPG * g + TPG)
                    for t in range(TPG):
                        last = pe.transpose(bank("x", k)[:, t * P:(t + 1) * P], xn[:, t, k * P:(k + 1) * P],
                                            ident[:, :])
                    last.then_inc(ring.done, 1)
                ring.copied(pe, g, U["x", 1])
                for name, col in (("u", 0), ("g", DI)):
                    for f in range(IT):
                        ring.free(pe, g, U[name, f])
                        more = left_out if (name, f) == ("g", IT - 1) else 0
                        mm3(pe, bank(name, f)[:, 0:GT], [w_in_at(k, col + f * P) for k in range(KT)],
                            [(x_hi[:, k, :], x_lo[:, k, :]) for k in range(KT)]).then_inc(ring.done, 1 + more)

            def stage_b(g, left_out=0):
                pe.wait_ge(ucl_ready, IT * g + IT)
                for f in range(IT):
                    for name, col in (("b", 0), ("c", DI)):
                        ring.free(pe, g, U[name, f])
                        more = left_out if (name, f) == ("c", IT - 1) else 0
                        mm3(pe, bank(name, f)[:, 0:GT], [w_bc_at(k, col + f * P) for k in range(IT)],
                            [(uc_hi[:, k, :], uc_lo[:, k, :]) for k in range(IT)]).then_inc(ring.done, 1 + more)

            def stage_c(g):
                pe.wait_ge(yl_ready, IT * g + 1)
                for t in range(TPG):
                    use = U["o", t // 2]
                    if t != 1:
                        ring.free(pe, g, use)
                    last = mm3(pe, banks[:, use % DEPTH, (t % 2) * D:(t % 2 + 1) * D],
                               [(y_hi[:, k, t * P:(t + 1) * P], y_lo[:, k, t * P:(t + 1) * P]) for k in range(IT)],
                               [part(OUT0, k, D, 0, D) for k in range(IT)])
                    if t == 1:
                        last.then_inc(ring.done, 1)
                last.then_inc(ring.done, 1 + PADS)

            pe.sem_inc(ring.done, ring.n + A0)
            pe.wait_ge(w_in, W_ALL)
            pe.wait_ge(w_split, 1)
            stage_a(0, ring.count("P", C0, ring.n))
            with pe.Fori(1, NG) as g:
                stage_b(g)
                stage_a(g)
                stage_c(g)
            stage_b(NG, ring.count("P", A0, C0))
            stage_c(NG)

        @block.scalar
        def _(act):
            def read(g, name, arg, out, func=ACT.Identity, bias=0.0, scale=1.0):
                ring.filled(act, g, U[name, arg])
                act.activation(out, bank(name, arg)[:, 0:GT], func, bias=bias, scale=scale).then_inc(
                    ring.sems["A"], 1)

            def stage_a(g):
                for k in range(KT):
                    read(g, "x", k, x_hi[:, k, :])
                for f in range(IT):
                    ring.filled(act, g, U["u", f])
                    act.activation(u[:, f, :, DC - 1:], bank("u", f)[:, 0:GT].rearrange("p (b t) -> p b t", b=GB),
                                   ACT.Identity, bias=b_in[:, f:f + 1]).then_inc(ring.sems["A"], 1)
                for f in range(IT):
                    act.wait_ge(conv_chain, DC * (IT * g + f + 1))
                    act.activation(uc_hi[:, f, :], conv[:, f, :], ACT.Silu).then_inc(uc_ready, 1)
                    act.activation(conv[:, f, :], conv[:, f, :], ACT.Silu).then_inc(uc_ready, 1)
                    if f == 0:
                        act.wait_ge(y_ready, IT * g + 1)
                    read(g, "g", f, gate[:, f, :], ACT.Tanh, b_gate[:, f:f + 1], 0.5)

            def y_high(g, f):
                act.wait_ge(y_ready, IT * (g - 1) + f + 2)
                act.activation(y_hi[:, f, :], y[:, f, :], ACT.Identity).then_inc(yh_ready, 1)

            def stage_b(g, left_out=0):
                for f in range(IT):
                    ring.filled(act, g, U["b", f])
                    act.wait_ge(state_ready, IT * (g - 1) + f + 1)
                    act.activation(bt[:, f % 2, :], bank("b", f)[:, 0:GT], ACT.Identity,
                                   bias=b_bc[:, f:f + 1]).then_inc(
                        ring.sems["A"], 1 + (left_out if f == IT - 1 else 0))
                    if f:
                        y_high(g, f - 1)
                y_high(g, IT - 1)

            ring.credit(act, "A", ring.count("A", 0, A0))
            act.wait_ge(w_in, W_ALL)
            act.activation(decay1[:, :], log_decay[:, :], ACT.Tanh, scale=-0.5).then_inc(decay_act, 1)
            act.wait_ge(scaled, 1)
            act.activation(w_hi[:, :], w_raw[:, :], ACT.Identity).then_inc(w_hi_ready, 1)
            norm.scalar(act)
            act.wait_ge(tables, 1)
            stage_a(0)
            with act.Fori(1, NG) as g:
                stage_b(g)
                stage_a(g)
            stage_b(NG, ring.count("A", A0, C0))

        @block.vector
        def _(dve):
            def layernorm(g):
                for t in range(TPG):
                    norm.apply(dve, xn[:, t, :], g * TPG + t).then_inc(xn_ready, 1)

            def stage_a(g, left_out=0):
                layernorm(g)
                for k in range(KT):
                    ring.copied_by(dve, g, U["x", k], "A")
                    dve.tensor_tensor(x_lo[:, k, :], bank("x", k)[:, 0:GT], x_hi[:, k, :].bitcast(F32),
                                      ALU.subtract).then_inc(
                        ring.sems["D"], 1 + (left_out if k == KT - 1 else 0))
                for f in range(IT):
                    ring.copied_by(dve, g, U["u", f], "A")
                    out = conv[:, f, :].rearrange("p (b t) -> p b t", b=GB)
                    dve.wait_ge(ucl_ready, IT * g + f + 1)
                    for k in range(DC):
                        n = DC * (IT * g + f) + k
                        tap = u[:, f, :, k:k + S]
                        if k == 0:
                            ins = dve.tensor_scalar(out, tap, conv_w[:, f, 0:1], conv_b[:, f:f + 1], ALU.mult, ALU.add)
                        else:
                            dve.wait_ge(conv_chain, n)
                            ins = dve.scalar_tensor_tensor(out, tap, conv_w[:, f, k:k + 1], out, ALU.mult, ALU.add)
                        ins.then_inc(conv_chain, 1)

            def stage_b(g, left_out=0):
                for f in range(IT):
                    n = IT * (g - 1) + f
                    ring.copied_by(dve, g, U["b", f], "A")
                    dve.tensor_tensor_scan(state[:, f % 2, :], decay[:, f, :], bt[:, f % 2, :], 0.0, ALU.mult,
                                           ALU.add).then_inc(state_ready, 1)
                    ring.filled(dve, g, U["c", f])
                    dve.wait_ge(state_ready, n + 3)
                    if f == 0:
                        dve.wait_ge(yl_ready, IT * (g - 1) + 1)
                    dve.scalar_tensor_tensor(y[:, f, :], bank("c", f)[:, 0:GT], b_bc[:, IT + f:IT + f + 1],
                                             state[:, f % 2, :], ALU.add, ALU.mult).then_inc(
                        ring.sems["D"], 1 + (left_out if f == IT - 1 else 0))
                    ring.copied_by(dve, g, U["c", f], "D")
                    dve.scalar_tensor_tensor(y[:, f, :], gate[:, f, :], 1.0, y[:, f, :], ALU.add,
                                             ALU.mult).then_inc(y_ready, 1)

            def stage_c(g):
                for n in range(2):
                    tiles = slice(2 * n, min(2 * n + 2, TPG))
                    w = tiles.stop - tiles.start
                    ring.filled(dve, g, U["o", n])
                    dve.wait_ge(out_added, 2 * (g - 1) + n + 1)
                    dve.tensor_tensor(outb[:, tiles, :], bank("o", n)[:, 0:w * D].rearrange("p (t d) -> p t d", t=w),
                                      bout[:, :].unsqueeze(1).broadcast_to([P, w, D]),
                                      ALU.add).then_inc(ring.sems["D"], 1)

            ring.credit(dve, "D", ring.count("D", 0, A0))
            dve.sem_inc(state_ready, 2)
            dve.sem_inc(y_ready, 1)
            dve.wait_ge(w_in, W_ALL)
            dve.tensor_scalar(w_raw[:, OUT0:], w_raw[:, OUT0:], 0.5, None, ALU.mult).then_inc(scaled, 1)
            dve.tensor_scalar(b_gate[:, :], b_in[:, IT:2 * IT], 0.5, None, ALU.mult)
            dve.memset(u[:, :, :, :], 0.0)
            dve.wait_ge(decay_act, 1)
            dve.tensor_scalar(decay2[:, :], decay1[:, :], 0.5, 0.5, ALU.mult, ALU.add).then_inc(ready, 1)
            dve.wait_ge(ready, 1)
            dve.tensor_copy(decay[:, :, :], decay2[:, :].unsqueeze(2).broadcast_to([P, IT, GT])).then_inc(ready, 1)
            dve.wait_ge(ready, 2)
            dve.memset(decay[:, :, 0:GT:S], 0.0).then_inc(tables, 1)
            norm.vector(dve)
            stage_a(0, ring.count("D", C0, ring.n))
            with dve.Fori(1, NG) as g:
                stage_b(g)
                stage_a(g)
                stage_c(g)
            stage_b(NG, ring.count("D", A0, C0))
            stage_c(NG)

        @block.gpsimd
        def _(pool):
            def uc_low(g):
                for f in range(IT):
                    pool.wait_ge(uc_ready, 2 * (IT * g + f) + 2)
                    pool.tensor_tensor(uc_lo[:, f, :], conv[:, f, :], uc_hi[:, f, :].bitcast(F32),
                                       ALU.subtract).then_inc(ucl_ready, 1)

            def y_low(g):
                for f in range(IT):
                    pool.wait_ge(yh_ready, IT * (g - 1) + f + 1)
                    pool.tensor_tensor(y_lo[:, f, :], y[:, f, :], y_hi[:, f, :].bitcast(F32),
                                       ALU.subtract).then_inc(yl_ready, 1)

            def add_out(g):
                for n in range(2):
                    w = min(2, TPG - 2 * n)
                    ring.copied(pool, g, U["o", n])
                    tile = Hs[:, bass.ds((g - 1) * TPG + 2 * n, w), :]
                    pool.tensor_tensor(tile, outb[:, 2 * n:2 * n + w, :], tile, ALU.add).then_inc(out_added, 1)

            pool.sem_inc(out_added, 2)
            pool.sem_inc(yl_ready, 1)
            pool.sem_inc(ucl_ready, IT)
            pool.wait_ge(w_hi_ready, 1)
            pool.tensor_tensor(w_lo[:, :], w_raw[:, :], w_hi[:, :].bitcast(F32), ALU.subtract).then_inc(w_split, 1)
            uc_low(0)
            with pool.Fori(1, NG) as g:
                y_low(g)
                uc_low(g)
                add_out(g)
            y_low(NG)
            add_out(NG)



HALF_T = NT // 2
HALF_G = NG // 2
EB = 512
EBT = EB // P
BLOCKS = HALF_T // EBT
LAG = 2


def experts(nc, Hs, dram, tag, NE, R, func, routed_from):
    ctx = ExitStack()
    with ctx:
        mem = Mem(nc, ctx, tag)
        sb, sem = mem.sb, mem.sem
        norm = Norm(mem, Hs)
        WC = KT * FF + FT * D
        W2 = KT * FF
        PAR = min(NE, 2)
        w_raw = sb("w_raw", [P, WC // 2])
        w_hi = sb("w_hi", [P, PAR, WC], F32R)
        w_lo = sb("w_lo", [P, PAR, WC], F32R)
        r_hi = sb("r_hi", [P, KT, P], F32R)
        r_lo = sb("r_lo", [P, KT, P], F32R)
        r_bias = sb("r_bias", [P, 1])
        b1 = sb("b1", [P, NE, FT])
        b1_now = sb("b1_now", [P, 2, FT])
        b2 = sb("b2", [P, NE, D])
        one = sb("one", [P, 1])
        ident = sb("ident", [P, P])
        shared = sb("shared", [P, TPG * D + GT])
        xn = shared[:, 0:TPG * D].rearrange("p (t d) -> p t d", t=TPG)
        logitsT = shared[:, TPG * D:]
        outb = shared[:, 0:4 * D].rearrange("p (b c) -> p b c", b=2)
        xT_hi = sb("xT_hi", [P, KT, HALF_T * P], F32R)
        xT_lo = sb("xT_lo", [P, KT, HALF_T * P], F32R)
        hid = sb("hid", [P, 2, EB])
        hid_hi = sb("hid_hi", [P, 4, EB], F32R)
        hid_lo = sb("hid_lo", [P, 4, EB], F32R)
        r_raw = hid[:, 0, 0:KT * P].rearrange("p (k m) -> p k m", k=KT)
        logits = sb("logits", [P, HALF_T, R])
        prob = sb("prob", [P, HALF_T, R])
        above = sb("above", [P, HALF_T, R, R])
        rank = sb("rank", [P, HALF_T, R])
        total = sb("total", [P, HALF_T])
        inv = sb("inv", [P, HALF_T])
        weight = sb("weight", [P, HALF_T, NE])
        banks = mem.ps("banks", [P, 4, 512])
        acc = mem.ps("acc", [P, 4, 512])

        ring = Ring(sem("prep_done"), sem("prep_act"), sem("prep_dve"), ["AD", "AD", "A", "D"], 4)
        XU, LU, TU = (0, 1), 2, 3
        w_in = sem("w_in")
        raw_in = sem("raw_in")
        w_hi_ready = sem("w_hi_ready")
        w_split = sem("w_split")
        r_hi_ready = sem("r_hi_ready")
        r_split = sem("r_split")
        xn_ready = sem("xn_ready")
        gate_chain = sem("gate_chain")
        gate_exp = sem("gate_exp")
        b1_ready = sem("b1_ready")
        one_ready = sem("one_ready")
        h_done = sem("h_done")
        h_act = sem("h_act")
        h_lo = sem("h_lo")
        h_used = sem("h_used")
        out_read = sem("out_read")
        out_added = sem("out_added")
        USED0 = 2 * BLOCKS * FT + 4

        small = [(r_raw, dram[tag + "_router"]), (r_bias[:, :], dram[tag + "_router_b"]),
                 (b1[:, :, :], dram[tag + "_b1"]), (ident[:, :], dram["ident"]),
                 (b2[:, :, :], dram[tag + "_b2"].broadcast_to([P, NE, D]))]
        GATE_STEPS = 7 if routed_from is not None else 10
        CH = WC // 2
        block = ctx.enter_context(nc.Block())

        def over_experts(eng, half, body):
            if NE == 1:
                body(0, 0, half)
            else:
                with eng.Fori(0, NE // 2) as pair:
                    for par in range(2):
                        body(par, pair * 2 + par, pair * 2 + (half * NE + par))

        @block.sync
        def _(sp):
            for dst, src in small:
                sp.dma_start(dst, src).then_inc(w_in, 16)
            def load(e, n, part):
                sp.wait_ge(w_split, n * 2 + (part + 1))
                sp.dma_start(w_raw[:, :], dram[tag + "_w"][bass.ds(e, 1), :, part * CH:(part + 1) * CH].rearrange(
                    "e p c -> p (e c)")).then_inc(raw_in, 16)

            for half in range(2 if NE > 1 else 1):
                with sp.Fori(0, NE) as e:
                    load(e, e + half * NE, 0)
                    load(e, e + half * NE, 1)

        def constants_in(eng):
            eng.wait_ge(w_in, 16 * len(small))

        @block.gpsimd
        def _(pool):
            def split(slot, e, n):
                pool.wait_ge(h_used, n * (BLOCKS * FT) + (BLOCKS * FT + 4))
                for part in range(2):
                    cols = slice(part * CH, (part + 1) * CH)
                    pool.wait_ge(raw_in, n * 32 + 16 * (part + 1))
                    pool.tensor_tensor(w_hi[:, slot, cols], w_raw[:, :], one[:, 0:1].broadcast_to([P, CH]),
                                       ALU.mult).then_inc(w_hi_ready, 1)
                    pool.wait_ge(w_hi_ready, n * 2 + (part + 1))
                    pool.tensor_tensor(w_lo[:, slot, cols], w_raw[:, :], w_hi[:, slot, cols].bitcast(F32),
                                       ALU.subtract).then_inc(w_split, 1)

            pool.sem_inc(w_split, 1)
            pool.memset(one[:, :], 1.0).then_inc(one_ready, 1)
            pool.wait_ge(one_ready, 1)
            for half in range(2 if NE > 1 else 1):
                over_experts(pool, half, split)

        @block.tensor
        def _(pe):
            def prep(half):
                with pe.Fori(0, HALF_G) as g0:
                    g = g0 + half * HALF_G
                    for k in range(KT):
                        ring.free(pe, g, XU[k])
                        if k == 0:
                            pe.wait_ge(xn_ready, g * TPG + TPG)
                        for t in range(TPG):
                            last = pe.transpose(banks[:, XU[k], t * P:(t + 1) * P], xn[:, t, k * P:(k + 1) * P],
                                                ident[:, :])
                        last.then_inc(ring.done, 1)
                    ring.free(pe, g, LU)
                    for k in range(KT):
                        ring.copied(pe, g, XU[k])
                    cols = bass.ds(g0 * GT, GT)
                    mm3(pe, banks[:, LU, 0:GT], [(r_hi[:, k, :], r_lo[:, k, :]) for k in range(KT)],
                        [(xT_hi[:, k, cols], xT_lo[:, k, cols]) for k in range(KT)]).then_inc(ring.done, 1)
                    ring.free(pe, g, TU)
                    ring.copied(pe, g, LU)
                    for t in range(TPG):
                        last = pe.transpose(banks[:, TU, t * P:(t + 1) * P], logitsT[:, t * P:(t + 1) * P], ident[:, :])
                    last.then_inc(ring.done, 1)
                for use in (XU[0], XU[1], LU, TU):
                    ring.copied(pe, half * HALF_G + HALF_G - 1, use)

            def first(slot, block_no, f):
                cols = bass.ds(block_no * EB, EB)
                mm3(pe, banks[:, f % 4, :],
                    [(w_hi[:, slot, k * FF + f * P:k * FF + (f + 1) * P],
                      w_lo[:, slot, k * FF + f * P:k * FF + (f + 1) * P]) for k in range(KT)],
                    [(xT_hi[:, k, cols], xT_lo[:, k, cols]) for k in range(KT)]).then_inc(h_done, 1)

            def second(slot, n, parity, f):
                pe.wait_ge(h_lo, n * FT + (f + 1 + 2))
                if f == 0:
                    pe.wait_ge(out_read, n * 2 + 2)
                rhs = (w_hi[:, slot, W2 + f * D:W2 + (f + 1) * D], w_lo[:, slot, W2 + f * D:W2 + (f + 1) * D])
                for t in range(EBT):
                    last = mm3(pe, acc[:, 2 * parity + t // 2, (t % 2) * D:(t % 2 + 1) * D],
                               [(hid_hi[:, f % 4, t * P:(t + 1) * P], hid_lo[:, f % 4, t * P:(t + 1) * P])], [rhs],
                               start=f == 0 and t % 2 == 0, stop=f == FT - 1, skip=True)
                last.then_inc(h_used, 1)

            def expert(slot, e, n):
                pe.wait_ge(w_split, n * 2 + 3 if NE > 1 else 3)

                def two_blocks(i, last=False):
                    for j in range(2 * FT):
                        second(slot, n * BLOCKS + i * 2 + j // FT, j // FT, j % FT)
                        ahead = j + LAG
                        if not last or ahead < 2 * FT:
                            first(slot, i * 2 + ahead // FT, ahead % FT)

                for f in range(LAG):
                    first(slot, 0, f)
                with pe.Fori(0, BLOCKS // 2 - 1) as i:
                    two_blocks(i)
                two_blocks(BLOCKS // 2 - 1, True)

            pe.sem_inc(ring.done, ring.n)
            pe.sem_inc(h_used, USED0)
            pe.wait_ge(w_in, 16 * len(small))
            pe.wait_ge(r_split, 1)
            for half in range(2):
                prep(half)
                over_experts(pe, half, expert)

        @block.scalar
        def _(act):
            def prep(half):
                with act.Fori(0, HALF_G) as g0:
                    g = g0 + half * HALF_G
                    for k in range(KT):
                        ring.filled(act, g, XU[k])
                        constants_in(act)
                        act.activation(xT_hi[:, k, bass.ds(g0 * GT, GT)], banks[:, XU[k], 0:GT],
                                       ACT.Identity).then_inc(ring.sems["A"], 1)
                    ring.filled(act, g, LU)
                    act.activation(logitsT, banks[:, LU, 0:GT], ACT.Identity,
                                   bias=r_bias[:, 0:1]).then_inc(ring.sems["A"], 1)

            def expert(slot, e, n):
                act.activation(b1_now[:, slot, :], b1[:, bass.ds(e, 1), :].rearrange("p e f -> p (e f)"),
                               ACT.Identity).then_inc(b1_ready, 1)
                act.wait_ge(b1_ready, n + 1)
                with act.Fori(0, BLOCKS // 2) as i:
                    for j in range(2 * FT):
                        f = j % FT
                        step = n * (BLOCKS * FT) + i * (2 * FT) + j
                        bias = b1_now[:, slot, f:f + 1]
                        act.wait_ge(h_done, step + 1)
                        act.wait_ge(h_used, step + (1 + USED0 - 4))
                        act.activation(hid_hi[:, f % 4, :], banks[:, f % 4, :], func, bias=bias).then_inc(h_act, 1)
                        act.wait_ge(h_lo, step + 1)
                        act.activation(hid[:, f % 2, :], banks[:, f % 4, :], func, bias=bias).then_inc(h_act, 1)

            ring.credit(act, "A")
            act.wait_ge(w_in, 16 * len(small))
            act.activation(r_hi[:, :, :], r_raw, ACT.Identity).then_inc(r_hi_ready, 1)
            norm.scalar(act)
            for half in range(2):
                prep(half)
                act.wait_ge(gate_chain, half * GATE_STEPS + 2)
                act.activation(prob[:, :, :], logits[:, :, :], ACT.Exp).then_inc(gate_exp, 1)
                over_experts(act, half, expert)

        @block.vector
        def _(dve):
            def prep(half):
                if half:
                    dve.wait_ge(out_added, NE * BLOCKS * 2 + 1)
                with dve.Fori(0, HALF_G) as g0:
                    g = g0 + half * HALF_G
                    ring.filled(dve, g, XU[1] - ring.n)
                    for t in range(TPG):
                        norm.apply(dve, xn[:, t, :], g * TPG + t).then_inc(xn_ready, 1)
                    for k in range(KT):
                        cols = bass.ds(g0 * GT, GT)
                        ring.copied_by(dve, g, XU[k], "A")
                        dve.tensor_tensor(xT_lo[:, k, cols], banks[:, XU[k], 0:GT], xT_hi[:, k, cols].bitcast(F32),
                                          ALU.subtract).then_inc(ring.sems["D"], 1)
                    ring.filled(dve, g, TU)
                    dve.tensor_scalar(logits[:, bass.ds(g0 * TPG, TPG), :],
                                      banks[:, TU, 0:GT].rearrange("p (t m) -> p t m", t=TPG)[:, :, 0:R],
                                      1.0, None, ALU.mult).then_inc(ring.sems["D"], 1)

            def gates(half):
                base = half * GATE_STEPS

                def over_classes(v):
                    return v.unsqueeze(2).broadcast_to([P, HALF_T, R])

                ring.copied(dve, half * HALF_G + HALF_G - 1, TU)
                dve.reduce_max(total[:, :], logits[:, :, :], AX.X).then_inc(gate_chain, 1)
                dve.wait_ge(gate_chain, base + 1)
                dve.tensor_tensor(logits[:, :, :], logits[:, :, :], over_classes(total[:, :]),
                                  ALU.subtract).then_inc(gate_chain, 1)
                dve.wait_ge(gate_exp, half + 1)
                dve.reduce_sum(total[:, :], prob[:, :, :], AX.X).then_inc(gate_chain, 1)
                dve.wait_ge(gate_chain, base + 3)
                dve.reciprocal(inv[:, :], total[:, :]).then_inc(gate_chain, 1)
                dve.wait_ge(gate_chain, base + 4)
                dve.tensor_tensor(prob[:, :, :], prob[:, :, :], over_classes(inv[:, :]), ALU.mult).then_inc(gate_chain, 1)
                dve.wait_ge(gate_chain, base + 5)
                for c in range(R):
                    for lo, hi, op in ((0, c, ALU.is_ge), (c + 1, R, ALU.is_gt)):
                        if lo < hi:
                            last = dve.tensor_tensor(above[:, :, c, lo:hi], prob[:, :, lo:hi],
                                                     prob[:, :, c:c + 1].broadcast_to([P, HALF_T, hi - lo]), op)
                last.then_inc(gate_chain, 1)
                dve.wait_ge(gate_chain, base + 6)
                dve.reduce_sum(rank[:, :, :], above[:, :, :, :], AX.X).then_inc(gate_chain, 1)
                dve.wait_ge(gate_chain, base + 7)
                if routed_from is not None:
                    dve.memset(weight[:, :, 0:routed_from], 1.0 / routed_from)
                    dve.scalar_tensor_tensor(weight[:, :, routed_from:], rank[:, :, :], 2.0, prob[:, :, :],
                                             ALU.is_lt, ALU.mult).then_inc(out_added, 1)
                else:
                    dve.scalar_tensor_tensor(prob[:, :, :], rank[:, :, :], 2.0, prob[:, :, :], ALU.is_lt,
                                             ALU.mult).then_inc(gate_chain, 1)
                    dve.wait_ge(gate_chain, base + 8)
                    dve.reduce_sum(total[:, :], prob[:, :, :], AX.X).then_inc(gate_chain, 1)
                    dve.wait_ge(gate_chain, base + 9)
                    dve.reciprocal(inv[:, :], total[:, :]).then_inc(gate_chain, 1)
                    dve.wait_ge(gate_chain, base + 10)
                    dve.tensor_tensor(weight[:, :, 0], total[:, :], inv[:, :], ALU.mult).then_inc(out_added, 1)

            def expert(slot, e, n, half):
                def read_out(i, bank):
                    dve.wait_ge(h_used, n * (BLOCKS * FT) + i * (2 * FT) + (bank // 2 + 1) * FT + USED0)
                    bias = b2[:, bass.ds(e, 1), :] if NE > 1 else b2[:, 0:1, :]
                    dve.tensor_tensor(outb[:, bank % 2, :].rearrange("p (t d) -> p t d", t=2),
                                      acc[:, bank, :].rearrange("p (t d) -> p t d", t=2),
                                      bias.broadcast_to([P, 2, D]), ALU.add).then_inc(out_read, 1)

                def add_to_h(i, bank):
                    dve.wait_ge(out_read, n * (2 * BLOCKS) + i * 4 + (bank + 1 + 4))
                    dve.wait_ge(out_added, n * (2 * BLOCKS) + i * 4 + (bank + 1 + half))
                    for t in range(2):
                        tile = i * (2 * EBT) + (2 * bank + t)
                        h = Hs[:, bass.ds(tile + half * HALF_T, 1), :].rearrange("p t d -> p (t d)")
                        wt = weight[:, bass.ds(tile, 1), bass.ds(e, 1) if NE > 1 else slice(0, 1)].rearrange(
                            "p t e -> p (t e)")
                        last = dve.scalar_tensor_tensor(h, outb[:, bank % 2, t * D:(t + 1) * D], wt, h,
                                                        ALU.mult, ALU.add)
                    last.then_inc(out_added, 1)

                def two_blocks(i, first=False):
                    for j in range(2 * FT):
                        step = n * (BLOCKS * FT) + i * (2 * FT) + j
                        dve.wait_ge(h_act, step * 2 + 2)
                        dve.tensor_tensor(hid_lo[:, j % 4, :], hid[:, j % 2, :], hid_hi[:, j % 4, :].bitcast(F32),
                                          ALU.subtract).then_inc(h_lo, 1)
                        if j in (2, 3) and not first:
                            read_out(i - 1, j)
                        if j in (4, 5) and not first:
                            add_to_h(i - 1, j - 2)
                        if j - FT in (2, 3):
                            read_out(i, j - FT - 2)
                        if j - FT in (4, 5):
                            add_to_h(i, j - FT - 4)

                two_blocks(0, True)
                with dve.Fori(1, BLOCKS // 2) as i:
                    two_blocks(i)
                for bank in (2, 3):
                    read_out(BLOCKS // 2 - 1, bank)
                for bank in (2, 3):
                    add_to_h(BLOCKS // 2 - 1, bank)

            ring.credit(dve, "D")
            dve.sem_inc(h_lo, 2)
            dve.sem_inc(out_read, 4)
            dve.memset(above[:, :, :, :].rearrange("p t a b -> p t (a b)")[:, :, 0:R * R:R + 1], 0.0)
            dve.wait_ge(r_hi_ready, 1)
            dve.tensor_tensor(r_lo[:, :, :], r_raw, r_hi[:, :, :].bitcast(F32), ALU.subtract).then_inc(r_split, 1)
            norm.vector(dve)
            for half in range(2):
                prep(half)
                gates(half)
                over_experts(dve, half, lambda slot, e, n: expert(slot, e, n, half))



def build(nc, dram, out):
    ctx = ExitStack()
    with ctx:
        Hs = ctx.enter_context(nc.sbuf_tensor("residual", [P, NT, D], F32))
        attention(nc, Hs, dram, False)
        recurrence(nc, Hs, dram)
        experts(nc, Hs, dram, "moe", SHARED + ROUTED, ROUTED, ACT.Relu, SHARED)
        attention(nc, Hs, dram, True)
        experts(nc, Hs, dram, "ffn", 1, CLASSES, ACT.Gelu_apprx_tanh, None)
        stored = ctx.enter_context(nc.semaphore("stored"))
        with nc.Block() as block:
            @block.sync
            def _(sp):
                sp.dma_start(out.rearrange("(t p) d -> p t d", p=P), Hs[:, :, :]).then_inc(stored, 16)
                sp.wait_ge(stored, 16)


def kernel(**inputs):
    import numpy as np
    import concourse.bacc as bacc
    from concourse.bass_utils import run_bass_kernel_spmd as run

    a = {k: np.asarray(v) for k, v in inputs.items()}

    def rows(w):
        return w.reshape(w.shape[0] // P, P, w.shape[1]).transpose(1, 0, 2)

    arrays = {}
    x = a["x"].reshape(NG, GB, M3, 4, KT, P)
    arrays["x"] = x.transpose(0, 5, 4, 3, 1, 2).reshape(NG, P, KT, 4, GB * M3)
    arrays["w_tok"] = rows(np.concatenate([a["L0_tok_Wqkv"].T, a["L0_tok_Wproj"].T], axis=1))
    arrays["ident"] = np.eye(P, dtype=np.float32)
    even = (np.arange(P) // DH % 2 == 0)
    for name, scale in (("masks_tok", D ** -0.5), ("masks_rel", DH ** -0.5)):
        arrays[name] = np.stack([even, ~even], axis=1).astype(np.float32) * np.float32(scale)
    arrays["w_rel"] = rows(np.concatenate([a[f"L1_attn_{n}"].T for n in ("Wq", "Wk", "Wv", "Wo")], axis=1))
    arrays["rel_kT"] = a["L1_attn_rel_k_emb"].T
    arrays["rel_v"] = a["L1_attn_rel_v_emb"]
    arrays["b_o"] = a["L1_attn_b_o"].reshape(1, D)
    w_in, w_bc, w_out = (rows(a[f"L0_attn_{n}"]).reshape(P, -1) for n in ("W_in", "W_bc", "W_out"))
    arrays["w_rc"] = np.concatenate([w_in, w_bc, w_out], axis=1)

    def column(v):
        return v.reshape(-1, P).T

    arrays["rc_b_in"] = column(a["L0_attn_b_in"])
    arrays["rc_conv_w"] = a["L0_attn_conv_w"].reshape(IT, P, DC).transpose(1, 0, 2)
    arrays["rc_conv_b"] = column(a["L0_attn_conv_b"])
    arrays["rc_b_bc"] = column(a["L0_attn_b_bc"])
    arrays["rc_log_decay"] = column(a["L0_attn_log_decay"])
    arrays["rc_b_out"] = a["L0_attn_b_out"].reshape(1, D)

    def expert_arrays(tag, w1, b1, w2, b2, router, router_b):
        n = w1.shape[0]
        arrays[tag + "_w"] = np.concatenate(
            [w1.reshape(n, KT, P, FF).transpose(0, 2, 1, 3).reshape(n, P, KT * FF),
             w2.reshape(n, FT, P, D).transpose(0, 2, 1, 3).reshape(n, P, FT * D)], axis=2)
        arrays[tag + "_b1"] = b1.reshape(n, FT, P).transpose(2, 0, 1)
        arrays[tag + "_b2"] = b2.reshape(1, n, D)
        arrays[tag + "_router"] = rows(np.pad(router, ((0, 0), (0, P - router.shape[1]))))
        arrays[tag + "_router_b"] = np.pad(router_b, (0, P - router_b.shape[0])).reshape(P, 1)

    def both(suffix):
        return np.concatenate([a["L0_ffn_s" + suffix], a["L0_ffn_r" + suffix]])

    expert_arrays("moe", both("w1"), both("b1"), both("w2"), both("b2"), a["L0_ffn_gate_w"], a["L0_ffn_gate_b"])
    expert_arrays("ffn", a["L1_ffn_w1"][None], a["L1_ffn_b1"][None], a["L1_ffn_w2"][None], a["L1_ffn_b2"][None],
                  a["L1_ffn_router_w"], np.zeros(CLASSES, np.float32))
    nc = bacc.Bacc("TRN2", target_bir_lowering=False, num_devices=1)
    arrays = {f"in_{k}": np.ascontiguousarray(v) for k, v in arrays.items()}
    dram = {k[3:]: nc.dram_tensor(k, v.shape, mybir.dt.from_np(v.dtype), kind="ExternalInput").ap()
            for k, v in arrays.items()}
    for name in ("skew_s", "skew_p"):
        dram[name] = nc.dram_tensor(name, (TPG, P, H, ROW), F32, kind="Internal").ap()
    out = nc.dram_tensor("out", (B * S, D), F32, kind="ExternalOutput").ap()
    build(nc, dram, out)
    got = run(nc, [arrays], core_ids=[0])
    return got.results[0]["out"].reshape(B, S, D)
```

```python
import concourse.bass as bass
from concourse import mybir
from contextlib import ExitStack

F32 = mybir.dt.float32
F32R = mybir.dt.float32r
ALU = mybir.AluOpType
ACT = mybir.ActivationFunctionType
AX = mybir.AxisListType

P = 128
B, S, D = 32, 192, 256
RAW_S = 256
H, DH = 16, 16
KT = D // P
GB = 2
GT = GB * S
TPG = GT // P
NG = B // GB
NT = B * S // P
HALF = 96
NJ = S // HALF
PAIRS = H // 2
M3 = S // 3
LN_EPS = 1e-5
DI = 512
IT = DI // P
DC = 4
FF = 1024
FT = FF // P
SHARED, ROUTED = 2, 4
CLASSES = 8
MAXREL = 32
QB = 64
WIN = QB + 2 * MAXREL
BAND = QB + 2 * MAXREL - 1
ROW = S


def mm3(pe, out, lhs, rhs, start=True, stop=True, skip=False):
    n = len(lhs)
    for k in range(n):
        (lh, ll), (rh, rl) = lhs[k], rhs[k]
        pe.matmul(out, lh, rh, start=start and k == 0, stop=False, skip_group_check=skip)
        pe.matmul(out, lh, rl, start=False, stop=False, skip_group_check=skip)
        last = pe.matmul(out, ll, rh, start=False, stop=stop and k == n - 1, skip_group_check=skip)
    return last


class Mem:

    def __init__(self, nc, ctx, tag):
        self.nc, self.ctx, self.tag = nc, ctx, tag

    def sb(self, name, shape, dt=F32):
        return self.ctx.enter_context(self.nc.sbuf_tensor(f"{self.tag}_{name}", shape, dt))

    def ps(self, name, shape):
        return self.ctx.enter_context(self.nc.psum_tensor(f"{self.tag}_{name}", shape, F32))

    def sem(self, name):
        return self.ctx.enter_context(self.nc.semaphore(f"{self.tag}_{name}"))


class Ring:

    def __init__(self, done, act, dve, readers, depth):
        self.done, self.sems, self.readers, self.depth = done, {"A": act, "D": dve}, readers, depth
        self.n = len(readers)
        self.lone, self.lacks = None, {}

    def alone(self, g, first):
        self.lone = g
        self.lacks = {letter: self.count(letter, 0, first) for letter in "PAD"}

    def lack(self, g, use, letter):
        if self.lone is None or g * self.n + use < self.lone * self.n:
            return 0
        return self.lacks[letter]

    def credit(self, eng, letter, more=0):
        eng.sem_inc(self.sems[letter], self.depth + more)

    def count(self, letter, first, last):
        return last - first if letter == "P" else sum(letter in r for r in self.readers[first:last])

    def upto(self, letter, use):
        if use >= 0:
            return sum(letter in r for r in self.readers[:use + 1])
        return -sum(letter in r for r in self.readers[self.n + use + 1:])

    def filled(self, eng, g, use):
        eng.wait_ge(self.done, g * self.n + (use + 1 + self.n - self.lack(g, use, "P")))

    def copied_by(self, eng, g, use, letter):
        per = sum(letter in r for r in self.readers)
        eng.wait_ge(self.sems[letter], g * per + (self.upto(letter, use) + self.depth - self.lack(g, use, letter)))

    def copied(self, eng, g, use):
        for letter in self.readers[use]:
            self.copied_by(eng, g, use, letter)

    def free(self, eng, g, use):
        self.copied(eng, g, use - self.depth)


class Norm:

    def __init__(self, mem, Hs):
        self.Hs = Hs
        self.stats = mem.sb("stats", [P, NT, 6])
        self.meanvar = mem.sb("meanvar", [P, NT, 2])
        self.vareps = mem.sb("vareps", [P, NT])
        self.std = mem.sb("std", [P, NT])
        self.y0 = mem.sb("y0", [P, NT])
        self.newton = mem.sb("newton", [P, NT])
        self.rstd = mem.sb("rstd", [P, NT])
        self.chain = mem.sem("norm_chain")
        self.root = mem.sem("norm_root")

    def vector(self, dve):
        for t in range(NT):
            last = dve.bn_stats(self.stats[:, t, :], self.Hs[:, t, :])
        last.then_inc(self.chain, 1)
        dve.wait_ge(self.chain, 1)
        for t in range(NT):
            last = dve.bn_aggr(self.meanvar[:, t, :], self.stats[:, t, :])
        last.then_inc(self.chain, 1)
        dve.wait_ge(self.chain, 2)
        dve.tensor_scalar(self.vareps[:, :], self.meanvar[:, :, 1], LN_EPS, None, ALU.add).then_inc(self.chain, 1)
        dve.wait_ge(self.root, 1)
        dve.reciprocal(self.y0[:, :], self.std[:, :]).then_inc(self.chain, 1)
        dve.wait_ge(self.chain, 4)
        dve.tensor_tensor(self.newton[:, :], self.y0[:, :], self.y0[:, :], ALU.mult).then_inc(self.chain, 1)
        dve.wait_ge(self.chain, 5)
        dve.tensor_tensor(self.newton[:, :], self.newton[:, :], self.vareps[:, :], ALU.mult).then_inc(self.chain, 1)
        dve.wait_ge(self.chain, 6)
        dve.tensor_scalar(self.newton[:, :], self.newton[:, :], -0.5, 1.5, ALU.mult, ALU.add).then_inc(self.chain, 1)
        dve.wait_ge(self.chain, 7)
        dve.tensor_tensor(self.rstd[:, :], self.y0[:, :], self.newton[:, :], ALU.mult).then_inc(self.chain, 1)
        dve.wait_ge(self.chain, 8)

    def scalar(self, act):
        act.wait_ge(self.chain, 3)
        act.activation(self.std[:, :], self.vareps[:, :], ACT.Sqrt).then_inc(self.root, 1)

    def apply(self, dve, out, n):
        one = bass.ds(n, 1)
        return dve.tensor_scalar(out, self.Hs[:, one, :].rearrange("p t d -> p (t d)"),
                                 self.meanvar[:, one, 0], self.rstd[:, one], ALU.subtract, ALU.mult)



PARTS = {0: [(0, P, 0)], 1: [(0, QB, 0), (QB, QB, 1)], 2: [(0, P, 1)]}
THIRD = {0: (0, 1), 1: (2, 0), 2: (1, 2)}


def window(third):
    first = QB * third - MAXREL
    return max(first, 0), min(first + WIN, S), max(-first, 0)


def attention(nc, Hs, dram, rel):
    ctx = ExitStack()
    with ctx:
        mem = Mem(nc, ctx, "a1" if rel else "a0")
        sb, sem = mem.sb, mem.sem
        w_raw = sb("w_raw", [P, KT, 4 * D])
        w_hi = sb("w_hi", [P, KT, 4 * D], F32R)
        w_lo = sb("w_lo", [P, KT, 4 * D], F32R)
        ident = sb("ident", [P, P])
        masks = sb("masks", [P, 2])
        if rel:
            norm = Norm(mem, Hs)
            xn = sb("xn", [P, TPG, D])
            x_hi = sb("x_hi", [P, KT, GT], F32R)
            x_lo = sb("x_lo", [P, KT, GT], F32R)
            relk = sb("relk", [P, 2 * MAXREL + 1])
            relkd = sb("relkd", [P, PAIRS // KT, 2 * MAXREL])
            relv = sb("relv", [P, DH])
            relv0 = sb("relv0", [P, DH])
            relvd = sb("relvd", [P, 2, 2 * DH])
            relv0_col = sb("relv0_col", [P, 1])
            rband = sb("rband", [P, 2, H, BAND + 1])
            swin = sb("swin", [P, 2, H, WIN])
            punsk = sb("punsk", [P, H, BAND + 1])
            puT = sb("puT", [P, 2, 4, P])
            bout = sb("bout", [P, D])
            outb = sb("outb", [P, D])
        else:
            xg = sb("xg", [P, 2, KT, 4, P])
            zero_row = sb("zero_row", [P, ROW])
            vT = sb("vT", [P, KT, GT])
        q_even = sb("q_even", [P, KT, GT])
        q_odd = sb("q_odd", [P, KT, GT])
        kT = sb("kT", [P, KT, GT])
        v = sb("v", [HALF, GB, NJ, 2, D])
        ctxraw = sb("ctxraw", [P, 2, D])
        probs = sb("probs", [P, 2, H, S])
        negmax = sb("negmax", [P, 4, 2])
        sums = sb("sums", [P, 2, H])
        rsum = sb("rsum", [P, H])
        rinv = sb("rinv", [P, 2, D])
        pT = sb("pT", [HALF, 2, 2, NJ, P])
        ctxn = sb("ctxn", [P, D])
        c_hi = sb("c_hi", [P, KT, P], F32R)
        c_lo = sb("c_lo", [P, KT, P], F32R)
        NSB = 3
        scores = mem.ps("scores", [P, NSB, 512])
        trans = mem.ps("trans", [P, 2, 512])
        ctxp = mem.ps("ctxp", [P, 512])
        proj = mem.ps("proj", [P, 2, 512])
        STEPS = TPG * PAIRS
        QUADS = H // 4

        if rel:
            LATE = {"rv": (2,), "c": (1, 2), "o": (1, 2)}
            puses = [("x", 0, "AD"), ("x", 1, "AD"), ("q", 0, "A"), ("q", 1, "D"), ("k", 0, "A"), ("k", 1, "D"),
                     ("r", (0, 0), "A"), ("r", (0, 1), "A"), ("v", 0, "A"), ("v", 1, "D"),
                     ("r", (1, 0), "A"), ("r", (1, 1), "A")]
            PLATE = len(puses)
            puses += [("c", 1, "D"), ("o", 1, "D"), ("rv", 2, "D"), ("c", 2, "D"), ("o", 2, "D")]
            PEARLY = len(puses)
            puses += [("r", (2, 0), "A"), ("r", (2, 1), "A")]
            puses += [("rv", 0, "D"), ("c", 0, "D"), ("o", 0, "D"), ("rv", 1, "D")]
            puses += [("pad", 0, "")]
        else:
            LATE = {"c": (2,), "o": (2,)}
            puses = [("q", 0, "A"), ("q", 1, "D"), ("k", 0, "A"), ("k", 1, "D"), ("vT", 0, "A"), ("vT", 1, "D"),
                     ("v", 0, "A"), ("v", 1, "D")]
            PLATE = len(puses)
            puses += [("c", 2, "D"), ("o", 2, "A")]
            PEARLY = len(puses)
            puses += [(name, t, r) for t in range(2) for name, r in (("c", "D"), ("o", "A"))]
        PU = {(name, arg): n for n, (name, arg, _) in enumerate(puses)}
        tuses = [("u", (TPG - 1, q), "A") for q in range(QUADS)] if rel else []
        TLATE = len(tuses)
        for s in range(STEPS):
            t, p = divmod(s, PAIRS)
            tuses.append(("s", s, "A" if rel and s % 2 else "D"))
            if rel and t and p >= QUADS:
                tuses.append(("u", (t - 1, p - QUADS), "A"))
        TU = {(name, arg): n for n, (name, arg, _) in enumerate(tuses)}
        proj_ring = Ring(sem("proj_done"), sem("proj_act"), sem("proj_dve"), [r for *_, r in puses], 2)
        trans_ring = Ring(sem("trans_done"), sem("trans_act"), sem("trans_dve"), [r for *_, r in tuses], 2)

        w_in = sem("w_in")
        w_hi_ready = sem("w_hi_ready")
        w_split = sem("w_split")
        x_in = [sem("x_in_even"), sem("x_in_odd")]
        xn_ready = sem("xn_ready")
        s_done = sem("s_done")
        rel_added = sem("rel_added")
        max_ready = sem("max_ready")
        p_ready = sem("p_ready")
        v_used = sem("v_used")
        ctx_out = sem("ctx_out")
        rs_ready = sem("rs_ready")
        rc_ready = sem("rc_ready")
        ch_ready = sem("ch_ready")
        cl_ready = sem("cl_ready")
        v_zeroed = sem("v_zeroed")
        out_added = sem("out_added")
        sw_in = sem("sw_in")
        r_out = sem("r_out")
        pw_out = sem("pw_out")
        pu_in = sem("pu_in")
        far_ready = sem("far_ready")
        rel_done = sem("rel_done")
        zeroed = sem("zeroed")
        table_zeroed = sem("table_zeroed")
        z_out = sem("z_out")
        P_CREDIT = 2 * NSB

        loads = [(w_raw[:, :, :], dram["w_rel" if rel else "w_tok"]), (ident[:, :], dram["ident"]),
                 (masks[:, :], dram["masks_rel" if rel else "masks_tok"])]
        if rel:
            loads += [(relk[DH * h:DH * (h + 1), :], dram["rel_kT"]) for h in range(P // DH)]
            loads += [(relv[0:2 * MAXREL, :], dram["rel_v"][1:2 * MAXREL + 1, :]),
                      (relv[2 * MAXREL:P, :],
                       dram["rel_v"][2 * MAXREL:2 * MAXREL + 1, :].broadcast_to([P - 2 * MAXREL, DH])),
                      (relv0[:, :], dram["rel_v"][0:1, :].broadcast_to([P, DH])),
                      (relv0_col[:, :], dram["rel_v0_col"]),
                      (bout[:, :], dram["b_o"].broadcast_to([P, D]))]
        W_ALL = 16 * len(loads)
        SPLITS = 3 if rel else 1

        def w(col, n, k):
            return (w_hi[:, k, col:col + n], w_lo[:, k, col:col + n])

        def slot(half, t):
            return (half * TPG + t) % 2

        def at(g, name, t):
            back, t = divmod(t, TPG)
            return g + (back + (t in LATE[name])), PU[name, t]

        def skipped(ring, letter, before):
            return ring.count(letter, PLATE, PEARLY) if before else 0

        def pair_rows(p):
            f, quad = divmod(p, PAIRS // KT)
            return f, slice(32 * quad, 32 * quad + 32)

        def bank_order(ap):
            return ap[:, 0:GT] if rel else ap[:, 0:GT].rearrange("p (r b m) -> p r b m", r=3, b=GB)

        def token_order(ap):
            return ap if rel else ap.rearrange("p (b m r) -> p r b m", r=3, b=GB)

        def heads_v(b, e):
            return v[:, b, :, e, :].rearrange("k j (p e d) -> k j p e d", e=2, d=DH)[:, :, :, e, :]

        def bank_v(bank, e):
            return bank[0:HALF, :].rearrange("k (j p e d) -> k j p e d", j=NJ, e=2, d=DH)[:, :, :, e, :]

        def key_order(ap):
            return ap if rel else ap.rearrange("p (b r m) -> p r b m", r=3, b=GB)

        block = ctx.enter_context(nc.Block())

        @block.sync
        def _(sp):
            for dst, src in loads:
                sp.dma_start(dst, src).then_inc(w_in, 16)
            if not rel:
                for g in range(2):
                    sp.dma_start(xg[:, g, :, :, :], dram["x"][g, :, :, :, :]).then_inc(x_in[g], 16)
                sp.wait_ge(zeroed, 1)
                for buf in (dram["skew_s"], dram["skew_p"]):
                    for t in range(TPG):
                        sp.dma_start(buf[t, :, :, :], zero_row[:, :].unsqueeze(1).broadcast_to([P, H, ROW])
                                     ).then_inc(z_out, 16)
                with sp.Fori(0, NG // 2 - 1) as gg:
                    for half in range(2):
                        g = gg * 2 + half
                        proj_ring.filled(sp, g, PU["vT", 1])
                        sp.dma_start(xg[:, half, :, :, :],
                                     dram["x"][bass.ds(g + 2, 1), :, :, :, :].rearrange("g p k o m -> (g p) k o m")
                                     ).then_inc(x_in[half], 16)
                sp.wait_ge(z_out, 16 * 2 * TPG)
                return
            sp.sem_inc(r_out, 32)
            sp.sem_inc(pw_out, 64)

            def skew_scores(g, half, t):
                n = g * TPG + t
                proj_ring.copied(sp, g, PU["r", (t, 1)])
                sp.wait_ge(rel_added, PAIRS * n + PAIRS)
                sp.dma_start(dram["skew_s"][t, :, :, QB:QB + BAND + 1], rband[:, slot(half, t), :, :]
                             ).then_inc(r_out, 16)
                sp.wait_ge(r_out, 16 * n + 16 + 32)
                for part in range(2):
                    src = bass.AP(dram["skew_s"].tensor, (t * P + part * QB) * H * ROW + QB - 1,
                                  [[H * ROW - 1, QB], [ROW, H], [1, WIN]])
                    sp.dma_start(swin[part * QB:(part + 1) * QB, slot(half, t), :, :], src).then_inc(sw_in, 16)

            def unskew_probs(g, half, t):
                n = g * TPG + t
                sp.wait_ge(p_ready, H * n + H + P_CREDIT)
                for part in range(2):
                    k0, k1, x0 = window(THIRD[t][part])
                    rows = slice(part * QB, (part + 1) * QB)
                    sp.dma_start(dram["skew_p"][t, rows, :, x0:x0 + k1 - k0],
                                 probs[rows, slot(half, t), :, k0:k1]).then_inc(pw_out, 16)
                sp.wait_ge(pw_out, 32 * n + 32 + 64)
                sp.wait_ge(rel_done, QUADS * n + QUADS)
                for part in range(2):
                    src = bass.AP(dram["skew_p"].tensor, (t * P + part * QB) * H * ROW + 1,
                                  [[H * ROW + 1, QB], [ROW, H], [1, BAND]])
                    sp.dma_start(punsk[part * QB:(part + 1) * QB, :, 0:BAND], src).then_inc(pu_in, 16)

            with sp.Fori(0, NG // 2) as gg:
                for half in range(2):
                    g = gg * 2 + half
                    skew_scores(g, half, 0)
                    skew_scores(g, half, 1)
                    unskew_probs(g, half, 0)
                    skew_scores(g, half, 2)
                    unskew_probs(g, half, 1)
                    unskew_probs(g, half, 2)

        @block.tensor
        def _(pe):
            def project(g, half, first):
                if rel:
                    for k in range(KT):
                        use = PU["x", k]
                        proj_ring.free(pe, g, use)
                        if k == 0:
                            pe.wait_ge(xn_ready, TPG * g + TPG)
                        for t in range(TPG):
                            last = pe.transpose(proj[:, use % 2, t * P:(t + 1) * P], xn[:, t, k * P:(k + 1) * P],
                                                ident[:, :])
                        last.then_inc(proj_ring.done, 1)
                    proj_ring.copied(pe, g, PU["x", 1])
                else:
                    pe.wait_ge(x_in[half], (g - half) * 8 + 16)
                for n, name in enumerate(("q", "k", "v" if rel else "vT")):
                    if name == "v":
                        proj_ring.copied(pe, g, PU["q", 0])
                        proj_ring.copied(pe, g, PU["q", 1])
                        relscore(g, 0)
                    for f in range(KT):
                        use = PU[name, f]
                        proj_ring.free(pe, g, use)
                        out = proj[:, use % 2, :]
                        if not rel:
                            for r in range(3):
                                o, j = divmod(4 * r + n, 3)
                                c = j * D + f * P
                                for k in range(KT):
                                    last = pe.matmul(out[:, r * P:(r + 1) * P], w_raw[:, k, c:c + P],
                                                     xg[:, half, k, o, :], start=k == 0, stop=k == KT - 1)
                        elif name != "v":
                            last = mm3(pe, out[:, 0:GT], [w(n * D + f * P, P, k) for k in range(KT)],
                                       [(x_hi[:, k, :], x_lo[:, k, :]) for k in range(KT)])
                        else:
                            for j in range(NJ):
                                tok = slice(f * S + j * HALF, f * S + (j + 1) * HALF)
                                last = mm3(pe, out[0:HALF, j * D:(j + 1) * D],
                                           [(x_hi[:, k, tok], x_lo[:, k, tok]) for k in range(KT)],
                                           [w(n * D, D, k) for k in range(KT)])
                        last.then_inc(proj_ring.done, 1)
                if not rel:
                    proj_ring.copied(pe, g, PU["vT", 0])
                    proj_ring.copied(pe, g, PU["vT", 1])
                    for b in range(GB):
                        use = PU["v", b]
                        proj_ring.free(pe, g, use)
                        for j in range(NJ):
                            for k in range(KT):
                                c = (j * KT + k) * P
                                last = pe.transpose(proj[0:HALF, use % 2, c:c + P],
                                                    vT[:, k, b * S + j * HALF:b * S + (j + 1) * HALF], ident[:, :])
                        last.then_inc(proj_ring.done, 1 + skipped(proj_ring, "P", first and b == GB - 1))
                proj_ring.copied(pe, g, PU["v", 0])
                proj_ring.copied(pe, g, PU["v", 1])

            def score(g, s):
                t, p = divmod(s, PAIRS)
                f, rows = pair_rows(p)
                pe.wait_ge(p_ready, 2 * (g * STEPS + s + 1 - NSB) + P_CREDIT)
                for h, q in enumerate((q_even, q_odd)):
                    for p0, n, b in PARTS[t]:
                        last = pe.matmul(scores[p0:p0 + n, s % NSB, h * S:(h + 1) * S],
                                         q[rows, f, t * P + p0:t * P + p0 + n],
                                         kT[rows, f, b * S:(b + 1) * S], start=True, stop=True)
                last.then_inc(s_done, 1)

            def turn(g, half, s):
                t, p = divmod(s, PAIRS)
                use = TU["s", s]
                trans_ring.free(pe, g, use)
                pe.wait_ge(p_ready, 2 * (g * STEPS + s + 1) + P_CREDIT)
                for h in range(2):
                    for j in range(NJ):
                        c = (h * NJ + j) * P
                        last = pe.transpose(trans[0:HALF, use % 2, c:c + P],
                                            probs[:, slot(half, t), 2 * p + h, j * HALF:(j + 1) * HALF],
                                            ident[:, :])
                last.then_inc(trans_ring.done, 1)

            def values(g, s):
                t, p = divmod(s, PAIRS)
                if p == 0:
                    pe.wait_ge(ctx_out, g * TPG + t + 1)
                trans_ring.copied(pe, g, TU["s", s])
                f, rows = pair_rows(p)
                for p0, n, b in PARTS[t]:
                    for h in range(2):
                        for j in range(NJ):
                            last = pe.matmul(ctxp[rows, f * P + p0:f * P + p0 + n],
                                             v[:, b, j, h, 2 * p * DH:2 * (p + 1) * DH], pT[:, s % 2, h, j, p0:p0 + n],
                                             start=(h == 0 and j == 0), stop=(h == 1 and j == NJ - 1))
                last.then_inc(v_used, 1)

            def relscore(g, t, first=False):
                for part in range(2):
                    use = PU["r", (t, part)]
                    proj_ring.free(pe, g, use)
                    for odd, q in enumerate((q_even, q_odd)):
                        c = odd * (PAIRS // KT) * 2 * MAXREL
                        last = pe.matmul(proj[:, use % 2, c:c + (PAIRS // KT) * 2 * MAXREL],
                                         q[:, part, t * P:(t + 1) * P],
                                         relkd[:, :, :].rearrange("p a r -> p (a r)"), start=True, stop=True)
                    last.then_inc(proj_ring.done, 1 + skipped(proj_ring, "P", first and part == 1))

            def relturn(g, t, quad):
                use = TU["u", (t, quad)]
                trans_ring.free(pe, g + (t == 2), use)
                if quad == 0:
                    pe.wait_ge(pu_in, 32 * (g * TPG + t) + 32)
                    pe.wait_ge(far_ready, g * TPG + t + 1 + 2)
                for i in range(4):
                    last = pe.transpose(trans[:, use % 2, i * P:(i + 1) * P], punsk[:, 4 * quad + i, :],
                                        ident[:, :])
                last.then_inc(trans_ring.done, 1)

            def relvalues(g, t, quad):
                r, use = at(g, "rv", t)
                if quad == 0:
                    proj_ring.free(pe, r, use)
                trans_ring.copied(pe, g + (t == 2), TU["u", (t, quad)])
                for i in range(4):
                    f, rows = pair_rows(2 * quad + i // 2)
                    last = pe.matmul(proj[rows, use % 2, f * P:(f + 1) * P], relvd[:, i % 2, :], puT[:, quad % 2, i, :],
                                     start=i % 2 == 0, stop=i % 2 == 1)
                    if quad == QUADS - 1 and i == 2:
                        last.then_inc(proj_ring.done, 2 if t == 1 else 1)
                last.then_inc(rel_done, 1)

            def turn_rinv(g, half, t):
                r, use = at(g, "c", t)
                proj_ring.free(pe, r, use)
                pe.wait_ge(rc_ready, g * TPG + t + 1)
                for k in range(KT):
                    last = pe.transpose(proj[:, use % 2, k * P:(k + 1) * P],
                                        rinv[:, slot(half, t), k * P:(k + 1) * P], ident[:, :])
                last.then_inc(proj_ring.done, 1)

            def project_out(g, t):
                r, use = at(g, "o", t)
                proj_ring.free(pe, r, use)
                pe.wait_ge(cl_ready, g * TPG + t + 3)
                mm3(pe, proj[:, use % 2, 0:D], [(c_hi[:, k, :], c_lo[:, k, :]) for k in range(KT)],
                    [w(3 * D, D, k) for k in range(KT)]).then_inc(proj_ring.done, 1)

            pe.sem_inc(proj_ring.done, proj_ring.n)
            pe.sem_inc(trans_ring.done, trans_ring.n + TLATE)
            if rel:
                pe.sem_inc(rel_done, QUADS)
            pe.wait_ge(w_in, W_ALL)
            pe.wait_ge(w_split, SPLITS)

            def late(g, half):
                if rel:
                    turn_rinv(g, half, 1)
                    relturn(g, 2, 0)
                    relturn(g, 2, 1)
                    project_out(g, 1)
                    for quad in range(QUADS):
                        relvalues(g, 2, quad)
                        if quad + 2 < QUADS:
                            relturn(g, 2, quad + 2)
                turn_rinv(g, half, 2)

            def two_groups(gg, first=False):
                for half in range(2):
                    g = gg * 2 + half
                    alone = first and half == 0
                    project(g, half, alone)
                    if rel:
                        relscore(g, 1, alone)
                    score(g, 0)
                    score(g, 1)
                    if not alone:
                        late(g - 1, 1 - half)
                    for s in range(STEPS):
                        t, p = divmod(s, PAIRS)
                        if s + 2 < STEPS:
                            score(g, s + 2)
                        turn(g, half, s)
                        if s == 3 and not alone:
                            project_out(g - 1, 2)
                        if s >= 1:
                            values(g, s - 1)
                        if rel and (t, p) == (2, 4):
                            project_out(g, 0)
                        if rel and t:
                            if p >= QUADS:
                                relturn(g, t - 1, p - QUADS)
                            if p > QUADS:
                                relvalues(g, t - 1, p - QUADS - 1)
                        if rel and (t, p) == (1, 1):
                            relscore(g, 2)
                        if rel and (t, p) == (2, 0):
                            relvalues(g, 0, QUADS - 1)
                            turn_rinv(g, half, 0)
                        if t and not rel and p == 2:
                            turn_rinv(g, half, t - 1)
                        if t and not rel and p == 5:
                            project_out(g, t - 1)
                    values(g, STEPS - 1)
                    if rel:
                        relvalues(g, 1, QUADS - 1)

            two_groups(0, True)
            with pe.Fori(1, NG // 2) as gg:
                two_groups(gg)
            for letter in "AD":
                proj_ring.copied_by(pe, NG - 1, proj_ring.n - 1, letter)
            proj_ring.alone(NG, PLATE)
            late(NG - 1, 1)
            project_out(NG - 1, 2)
            proj_ring.alone(None, 0)

        @block.scalar
        def _(act):
            proj_ring.credit(act, "A")
            trans_ring.credit(act, "A", TLATE)
            act.sem_inc(p_ready, P_CREDIT)
            if rel:
                norm.scalar(act)
            act.wait_ge(v_zeroed, 1)
            act.wait_ge(w_in, W_ALL)
            act.activation(w_hi[:, :, :], w_raw[:, :, :], ACT.Identity).then_inc(w_hi_ready, 1)

            def bank_of(name, arg):
                return proj[:, PU[name, arg] % 2, :]

            def copy(g, name, arg, out, src, scale=1.0):
                proj_ring.filled(act, g, PU[name, arg])
                act.activation(out, src, ACT.Identity, scale=scale).then_inc(proj_ring.sems["A"], 1)

            def read_band(g, half, t, first=False):
                n = g * TPG + t
                act.wait_ge(r_out, 16 * n + 16)
                act.wait_ge(rel_added, PAIRS * n + PAIRS)
                for part in range(2):
                    proj_ring.filled(act, g, PU["r", (t, part)])
                    bank = bank_of("r", (t, part)).rearrange("p (e a r) -> p a e r", e=2, r=2 * MAXREL)
                    band = rband[:, slot(half, t), part * H // 2:(part + 1) * H // 2, :].rearrange(
                        "p (a e) r -> p a e r", e=2)
                    act.activation(band[:, :, :, 0:2 * MAXREL], bank, ACT.Identity)
                    act.activation(band[:, :, :, 2 * MAXREL:BAND + 1], bank[:, :, :, 2 * MAXREL - 1:2 * MAXREL].broadcast_to(
                        [P, PAIRS // KT, 2, BAND + 1 - 2 * MAXREL]), ACT.Identity).then_inc(
                        proj_ring.sems["A"], 1 + skipped(proj_ring, "A", first and part == 1))

            def exponentials(g, half, s):
                t, p = divmod(s, PAIRS)
                if rel and p == 0:
                    act.wait_ge(pw_out, 32 * (g * TPG + t) + 32)
                    act.wait_ge(far_ready, g * TPG + t + 1)
                act.wait_ge(max_ready, g * STEPS + s + 1)
                for h in range(2):
                    act.activation(probs[:, slot(half, t), 2 * p + h, :], scores[:, s % NSB, h * S:(h + 1) * S],
                                   ACT.Exp, bias=negmax[:, s % 4, h:h + 1],
                                   accum_out=sums[:, slot(half, t), 2 * p + h:2 * p + h + 1]).then_inc(p_ready, 1)

            def copy_turned(g, s):
                use = TU["s", s]
                trans_ring.filled(act, g, use)
                act.activation(pT[:, s % 2, :, :, :].rearrange("k h j q -> k (h j q)"), trans[0:HALF, use % 2, :],
                               ACT.Identity).then_inc(trans_ring.sems["A"], 1)

            def copy_relturned(g, t, quad):
                use = TU["u", (t, quad)]
                trans_ring.filled(act, g + (t == 2), use)
                act.activation(puT[:, quad % 2, :, :].rearrange("r h q -> r (h q)"), trans[:, use % 2, :],
                               ACT.Identity).then_inc(trans_ring.sems["A"], 1)

            def split_ctx(g, t):
                proj_ring.filled(act, *at(g, "o", t - 1))
                proj_ring.copied(act, *at(g, "c", t))
                act.activation(c_hi[:, :, :].rearrange("p k q -> p (k q)"), ctxn[:, :], ACT.Identity,
                               bias=relv0_col[:, 0:1] if rel else 0.0).then_inc(ch_ready, 1)

            def store_out(g, t):
                copy(at(g, "o", t)[0], "o", t, Hs[:, bass.ds(g * TPG + t, 1), :].rearrange("p t d -> p (t d)"),
                     bank_of("o", t)[:, 0:D])

            def late(g):
                if rel:
                    split_ctx(g, 1)
                    for quad in range(QUADS):
                        copy_relturned(g, 2, quad)

            def two_groups(gg, first=False):
                for half in range(2):
                    g = gg * 2 + half
                    alone = first and half == 0
                    if rel:
                        for k in range(KT):
                            copy(g, "x", k, x_hi[:, k, :], bank_of("x", k)[:, 0:GT])
                    proj_ring.filled(act, g, PU["q", 0])
                    act.activation(token_order(q_even[:, 0, :]), bank_order(bank_of("q", 0)), ACT.Identity,
                                   scale=masks[:, 0:1])
                    copy(g, "q", 0, token_order(q_odd[:, 0, :]), bank_order(bank_of("q", 0)), masks[:, 1:2])
                    copy(g, "k", 0, key_order(kT[:, 0, :]), bank_order(bank_of("k", 0)))
                    if not rel:
                        copy(g, "vT", 0, key_order(vT[:, 0, :]), bank_order(bank_of("vT", 0)))
                    if rel:
                        read_band(g, half, 0)
                    proj_ring.filled(act, g, PU["v", 0])
                    for e in range(2):
                        last = act.activation(heads_v(0, e), bank_v(bank_of("v", 0), e), ACT.Identity)
                    last.then_inc(proj_ring.sems["A"], 1 + skipped(proj_ring, "A", alone and not rel))
                    if rel:
                        read_band(g, half, 1, alone)
                    if not alone:
                        late(g - 1)
                    for s in range(STEPS + 1):
                        t, p = divmod(s, PAIRS)
                        if s < STEPS:
                            exponentials(g, half, s)
                        if rel and s and (s - 1) % 2:
                            copy_turned(g, s - 1)
                        if rel and s - 1 >= PAIRS and (s - 1) % PAIRS >= QUADS:
                            copy_relturned(g, (s - 1) // PAIRS - 1, (s - 1) % PAIRS - QUADS)
                        if rel and (t, p) == (1, 2):
                            read_band(g, half, 2)
                        if rel and (t, p) == (2, 2):
                            split_ctx(g, 0)
                        if not rel and t in (1, 2):
                            if p == 4:
                                split_ctx(g, t - 1)
                            if p == 6:
                                store_out(g, t - 1)
                        if s == 1 and not alone:
                            split_ctx(g - 1, 2)
                        if not rel and s == 5 and not alone:
                            store_out(g - 1, 2)

            two_groups(0, True)
            with act.Fori(1, NG // 2) as gg:
                two_groups(gg)
            proj_ring.alone(NG, PLATE)
            late(NG - 1)
            split_ctx(NG - 1, 2)
            if not rel:
                store_out(NG - 1, 2)
            proj_ring.alone(None, 0)

        @block.vector
        def _(dve):
            proj_ring.credit(dve, "D")
            trans_ring.credit(dve, "D")
            dve.sem_inc(ctx_out, 1)
            dve.sem_inc(cl_ready, 2)
            dve.memset(v[:, :, :, :, :], 0.0).then_inc(v_zeroed, 1)
            if rel:
                norm.vector(dve)
            else:
                dve.memset(zero_row[:, :], 0.0).then_inc(zeroed, 1)
            dve.wait_ge(w_in, W_ALL)
            if rel:
                dve.sem_inc(rel_added, 2 * PAIRS)
                dve.sem_inc(far_ready, 2)
                dve.memset(relvd[:, :, :], 0.0)
                dve.memset(relkd[:, :, :], 0.0).then_inc(table_zeroed, 1)
                dve.wait_ge(table_zeroed, 1)
                for a in range(PAIRS // KT):
                    rows = slice(32 * a, 32 * a + 32)
                    last = dve.tensor_scalar(relkd[rows, a, :], relk[rows, 1:2 * MAXREL + 1], relk[rows, 0:1], None,
                                             ALU.subtract)
                last.then_inc(w_split, 1)
                for e in range(2):
                    last = dve.tensor_tensor(relvd[:, e, e * DH:(e + 1) * DH], relv[:, :], relv0[:, :], ALU.subtract)
                last.then_inc(w_split, 1)

            def bank_of(name, arg):
                return proj[:, PU[name, arg] % 2, :]

            def done(ins):
                ins.then_inc(proj_ring.sems["D"], 1)

            def copy(g, name, arg, out, src):
                proj_ring.filled(dve, g, PU[name, arg])
                done(dve.tensor_copy(out, src))

            def layernorm(g):
                for t in range(TPG):
                    norm.apply(dve, xn[:, t, :], g * TPG + t).then_inc(xn_ready, 1)

            def maxima(g, half, s):
                t, p = divmod(s, PAIRS)
                bank = scores[:, s % NSB, 0:2 * S].rearrange("q (h k) -> q h k", h=2)
                dve.wait_ge(s_done, g * STEPS + s + 1)
                if rel:
                    if p == 0:
                        dve.wait_ge(sw_in, 32 * (g * TPG + t) + 32)
                    for part in range(2):
                        k0, k1, x0 = window(THIRD[t][part])
                        rows = slice(part * QB, (part + 1) * QB)
                        last = dve.tensor_tensor(bank[rows, :, k0:k1],
                                                 swin[rows, slot(half, t), 2 * p:2 * p + 2, x0:x0 + k1 - k0],
                                                 bank[rows, :, k0:k1], ALU.add)
                        if k1 < S:
                            last = dve.tensor_tensor(bank[rows, :, k1:S],
                                                     rband[rows, slot(half, t), 2 * p:2 * p + 2, BAND - 1:BAND]
                                                     .broadcast_to([QB, 2, S - k1]), bank[rows, :, k1:S], ALU.add)
                    last.then_inc(rel_added, 1)
                    dve.wait_ge(rel_added, g * STEPS + s + 1 + 2 * PAIRS)
                dve.tensor_reduce(negmax[:, s % 4, :], bank, AX.X, ALU.max, negate=True).then_inc(max_ready, 1)

            def copy_turned(g, s):
                use = TU["s", s]
                trans_ring.filled(dve, g, use)
                dve.tensor_copy(pT[:, s % 2, :, :, :].rearrange("k h j q -> k (h j q)"), trans[0:HALF, use % 2, :]
                                ).then_inc(trans_ring.sems["D"], 1)

            def reciprocals(g, half, t):
                n = g * TPG + t
                dve.wait_ge(p_ready, H * (n + 1) + P_CREDIT)
                proj_ring.filled(dve, *at(g, "c", t - 2))
                dve.reciprocal(rsum[:, :], sums[:, slot(half, t), :]).then_inc(rs_ready, 1)
                dve.wait_ge(rs_ready, n + 1)
                dve.tensor_copy(rinv[:, slot(half, t), :].rearrange("p (h d) -> p h d", h=H),
                                rsum[:, :].unsqueeze(2).broadcast_to([P, H, DH])).then_inc(rc_ready, 1)

            def far_sums(g, half, t):
                n = g * TPG + t
                dve.wait_ge(rel_done, QUADS * n + QUADS)
                for part in range(2):
                    _, k1, _ = window(THIRD[t][part])
                    rows = slice(part * QB, (part + 1) * QB)
                    if k1 < S:
                        last = dve.tensor_reduce(punsk[rows, :, BAND], probs[rows, slot(half, t), :, k1:S],
                                                  AX.X, ALU.add)
                    else:
                        last = dve.memset(punsk[rows, :, BAND], 0.0)
                last.then_inc(far_ready, 1)

            def read_ctx(g, half, t):
                n = g * TPG + t
                dve.wait_ge(v_used, PAIRS * (n + 1))
                dve.wait_ge(cl_ready, n + 1)
                dve.tensor_copy(ctxraw[:, slot(half, t), :], ctxp[:, 0:D]).then_inc(ctx_out, 1)

            def sums_of(g, half, t):
                reciprocals(g, half, t)
                if rel:
                    far_sums(g, half, t)

            def add_rel(g, half, t):
                n = g * TPG + t
                dve.wait_ge(rel_done, QUADS * (n + 1) + QUADS)
                dve.wait_ge(ctx_out, n + 2)
                dve.wait_ge(cl_ready, n + 2)
                done(dve.tensor_tensor(ctxn[:, :], ctxraw[:, slot(half, t), :], bank_of("rv", t)[:, 0:D], ALU.add))

            def normalise(g, half, t):
                n = g * TPG + t
                if rel:
                    proj_ring.copied(dve, *at(g, "rv", t))
                    summed = ctxn[:, :]
                else:
                    dve.wait_ge(ctx_out, n + 2)
                    dve.wait_ge(cl_ready, n + 2)
                    summed = ctxraw[:, slot(half, t), :]
                proj_ring.filled(dve, *at(g, "c", t))
                done(dve.tensor_tensor(ctxn[:, :], summed, bank_of("c", t)[:, 0:D], ALU.mult))

            def split_ctx(g, t):
                proj_ring.copied(dve, *at(g, "c", t))
                dve.wait_ge(ch_ready, g * TPG + t + 1)
                hi, lo = (x[:, :, :].rearrange("p k q -> p (k q)") for x in (c_hi, c_lo))
                if rel:
                    ins = dve.scalar_tensor_tensor(lo, ctxn[:, :], relv0_col[:, 0:1], hi.bitcast(F32), ALU.add,
                                                   ALU.subtract)
                else:
                    ins = dve.tensor_tensor(lo, ctxn[:, :], hi.bitcast(F32), ALU.subtract)
                ins.then_inc(cl_ready, 1)

            def out_bias(g, t):
                dve.wait_ge(out_added, g * TPG + t + 1)
                proj_ring.filled(dve, *at(g, "o", t))
                done(dve.tensor_tensor(outb[:, :], bank_of("o", t)[:, 0:D], bout[:, :], ALU.add))

            def late(g, half):
                if rel:
                    normalise(g, half, 1)
                    split_ctx(g, 1)
                    out_bias(g, 1)
                    add_rel(g, half, 2)

            def two_groups(gg, first=False, final=False):
                for half in range(2):
                    g = gg * 2 + half
                    alone = first and half == 0
                    if rel:
                        for k in range(KT):
                            proj_ring.copied_by(dve, g, PU["x", k], "A")
                            done(dve.tensor_tensor(x_lo[:, k, :], bank_of("x", k)[:, 0:GT],
                                                   x_hi[:, k, :].bitcast(F32), ALU.subtract))
                    if not alone:
                        sums_of(g - 1, 1 - half, 2)
                    proj_ring.filled(dve, g, PU["q", 1])
                    dve.tensor_scalar(token_order(q_even[:, 1, :]), bank_order(bank_of("q", 1)), masks[:, 0:1],
                                      None, ALU.mult)
                    done(dve.tensor_scalar(token_order(q_odd[:, 1, :]), bank_order(bank_of("q", 1)), masks[:, 1:2],
                                           None, ALU.mult))
                    copy(g, "k", 1, key_order(kT[:, 1, :]), bank_order(bank_of("k", 1)))
                    if not rel:
                        copy(g, "vT", 1, key_order(vT[:, 1, :]), bank_order(bank_of("vT", 1)))
                    proj_ring.filled(dve, g, PU["v", 1])
                    for e in range(2):
                        last = dve.tensor_copy(heads_v(1, e), bank_v(bank_of("v", 1), e))
                    last.then_inc(proj_ring.sems["D"], 1 + skipped(proj_ring, "D", alone))
                    if not alone:
                        late(g - 1, 1 - half)
                    for s in range(STEPS + 1):
                        t, p = divmod(s, PAIRS)
                        if s < STEPS:
                            maxima(g, half, s)
                        if rel and (t, p) == (2, 6) and not (final and half):
                            layernorm(g + 1)
                        if s and not (rel and (s - 1) % 2):
                            copy_turned(g, s - 1)
                        if p == 1 and t:
                            read_ctx(g, half, t - 1)
                            sums_of(g, half, t - 1)
                            if rel and t == 2:
                                add_rel(g, half, 0)
                                normalise(g, half, 0)
                        if rel and (t, p) == (2, 2):
                            split_ctx(g, 0)
                        if rel and (t, p) == (2, 5):
                            out_bias(g, 0)
                        if not rel and t in (1, 2):
                            if p == 3:
                                normalise(g, half, t - 1)
                            if p == 4:
                                split_ctx(g, t - 1)
                        if s == 1 and not alone:
                            normalise(g - 1, 1 - half, 2)
                        if s == 2 and not alone:
                            split_ctx(g - 1, 2)
                        if rel and s == 5 and not alone:
                            out_bias(g - 1, 2)
                    read_ctx(g, half, 2)
                    if rel:
                        add_rel(g, half, 1)

            if rel:
                layernorm(0)
            two_groups(0, first=True)
            with dve.Fori(1, NG // 2 - 1) as gg:
                two_groups(gg)
            two_groups(NG // 2 - 1, final=True)
            proj_ring.alone(NG, PLATE)
            sums_of(NG - 1, 1, 2)
            late(NG - 1, 1)
            normalise(NG - 1, 1, 2)
            split_ctx(NG - 1, 2)
            if rel:
                out_bias(NG - 1, 2)
            proj_ring.alone(None, 0)

        @block.gpsimd
        def _(pool):
            pool.wait_ge(w_in, W_ALL)
            pool.wait_ge(w_hi_ready, 1)
            pool.tensor_tensor(w_lo[:, :, :], w_raw[:, :, :], w_hi[:, :, :].bitcast(F32),
                               ALU.subtract).then_inc(w_split, 1)
            if rel:
                pool.sem_inc(out_added, 1)
                def add_out(g, t):
                    tile = Hs[:, bass.ds(g * TPG + t, 1), :].rearrange("p t d -> p (t d)")
                    proj_ring.copied_by(pool, *at(g, "o", t), "D")
                    pool.tensor_tensor(tile, outb[:, :], tile, ALU.add).then_inc(out_added, 1)

                add_out(0, 0)
                with pool.Fori(0, NG - 1) as g:
                    add_out(g, 1)
                    add_out(g, 2)
                    add_out(g + 1, 0)
                proj_ring.alone(NG, PLATE)
                add_out(NG - 1, 1)
                add_out(NG - 1, 2)
                proj_ring.alone(None, 0)



def recurrence(nc, Hs, dram):
    ctx = ExitStack()
    with ctx:
        mem = Mem(nc, ctx, "rc")
        sb, sem = mem.sb, mem.sem
        norm = Norm(mem, Hs)
        NW = KT * 2 * DI + IT * 2 * DI + IT * D
        w_raw = sb("w_raw", [P, NW])
        w_hi = sb("w_hi", [P, NW], F32R)
        w_lo = sb("w_lo", [P, NW], F32R)
        OUT0 = KT * 2 * DI + IT * 2 * DI
        ident = sb("ident", [P, P])
        b_in = sb("b_in", [P, 2 * IT])
        b_gate = sb("b_gate", [P, IT])
        conv_w = sb("conv_w", [P, IT, DC])
        conv_b = sb("conv_b", [P, IT])
        b_bc = sb("b_bc", [P, 2 * IT])
        log_decay = sb("log_decay", [P, IT])
        decay1 = sb("decay1", [P, IT])
        decay2 = sb("decay2", [P, IT])
        decay = sb("decay", [P, IT, GT])
        bout = sb("bout", [P, D])
        xn = sb("xn", [P, TPG, D])
        x_hi = sb("x_hi", [P, KT, GT], F32R)
        x_lo = sb("x_lo", [P, KT, GT], F32R)
        u = sb("u", [P, IT, GB, DC - 1 + S])
        conv = sb("conv", [P, IT, GT])
        uc_hi = sb("uc_hi", [P, IT, GT], F32R)
        uc_lo = sb("uc_lo", [P, IT, GT], F32R)
        gate = sb("gate", [P, IT, GT])
        bt = sb("bt", [P, 2, GT])
        state = sb("state", [P, 2, GT])
        y = w_raw[:, 0:IT * GT].rearrange("p (f t) -> p f t", f=IT)
        y_hi = sb("y_hi", [P, IT, GT], F32R)
        y_lo = sb("y_lo", [P, IT, GT], F32R)
        outb = sb("outb", [P, TPG, D])
        DEPTH = 8
        banks = mem.ps("banks", [P, DEPTH, 512])

        uses = [("x", k, "AD") for k in range(KT)]
        B0 = len(uses)
        uses += [(name, f, r) for f in range(IT) for name, r in (("b", "A"), ("c", "D"))]
        A0 = len(uses)
        uses += [("u", f, "A") for f in range(IT)]
        uses += [("g", f, "A") for f in range(IT)]
        C0 = len(uses)
        uses += [("o", 0, "D"), ("o", 1, "D")]
        PADS = -len(uses) % DEPTH
        uses += [("pad", i, "") for i in range(PADS)]
        U = {(name, arg): n for n, (name, arg, _) in enumerate(uses)}
        ring = Ring(sem("done"), sem("act"), sem("dve"), [r for *_, r in uses], DEPTH)

        w_in = sem("w_in")
        w_rest_in = sem("w_rest_in")
        w_hi_ready = sem("w_hi_ready")
        w_in_split = sem("w_in_split")
        w_split = sem("w_split")
        ready = sem("ready")
        tables = sem("tables")
        decay_act = sem("decay_act")
        xn_ready = sem("xn_ready")
        conv_chain = sem("conv_chain")
        uc_ready = sem("uc_ready")
        ucl_ready = sem("ucl_ready")
        state_ready = sem("state_ready")
        y_ready = sem("y_ready")
        yh_ready = sem("yh_ready")
        yl_ready = sem("yl_ready")
        out_added = sem("out_added")

        IN = KT * 2 * DI
        loads = [(w_raw[:, 0:IN], dram["w_rc"][:, 0:IN]), (ident[:, :], dram["ident"]), (b_in[:, :], dram["rc_b_in"]),
                 (conv_w[:, :, :], dram["rc_conv_w"]), (conv_b[:, :], dram["rc_conv_b"]),
                 (b_bc[:, :], dram["rc_b_bc"]), (log_decay[:, :], dram["rc_log_decay"]),
                 (bout[:, :], dram["rc_b_out"].broadcast_to([P, D]))]
        W_ALL = 16 * len(loads)

        def part(base, k, width, col, n):
            c = base + k * width + col
            return (w_hi[:, c:c + n], w_lo[:, c:c + n])

        def w_in_at(k, col):
            return part(0, k, 2 * DI, col, P)

        def w_bc_at(k, col):
            return part(KT * 2 * DI, k, 2 * DI, col, P)

        def bank(name, arg):
            return banks[:, U[name, arg] % DEPTH, :]

        block = ctx.enter_context(nc.Block())

        @block.sync
        def _(sp):
            for dst, src in loads:
                sp.dma_start(dst, src).then_inc(w_in, 16)
            sp.dma_start(w_raw[:, IN:], dram["w_rc"][:, IN:]).then_inc(w_rest_in, 16)

        @block.tensor
        def _(pe):
            def stage_x(g, left_out=0):
                for k in range(KT):
                    ring.free(pe, g, U["x", k])
                    if k == 0:
                        pe.wait_ge(xn_ready, TPG * g + TPG)
                    for t in range(TPG):
                        last = pe.transpose(bank("x", k)[:, t * P:(t + 1) * P], xn[:, t, k * P:(k + 1) * P],
                                            ident[:, :])
                    last.then_inc(ring.done, 1 + (left_out if k == KT - 1 else 0))

            def stage_a(g, left_out=0):
                ring.copied(pe, g, U["x", 1])
                for name, col in (("u", 0), ("g", DI)):
                    for f in range(IT):
                        ring.free(pe, g, U[name, f])
                        more = left_out if (name, f) == ("g", IT - 1) else 0
                        mm3(pe, bank(name, f)[:, 0:GT], [w_in_at(k, col + f * P) for k in range(KT)],
                            [(x_hi[:, k, :], x_lo[:, k, :]) for k in range(KT)]).then_inc(ring.done, 1 + more)

            def stage_b(g, left_out=0):
                pe.wait_ge(ucl_ready, IT * g + IT)
                for f in range(IT):
                    for name, col in (("b", 0), ("c", DI)):
                        ring.free(pe, g, U[name, f])
                        more = left_out if (name, f) == ("c", IT - 1) else 0
                        mm3(pe, bank(name, f)[:, 0:GT], [w_bc_at(k, col + f * P) for k in range(IT)],
                            [(uc_hi[:, k, :], uc_lo[:, k, :]) for k in range(IT)]).then_inc(ring.done, 1 + more)

            def stage_c(g):
                pe.wait_ge(yl_ready, IT * g + 1)
                for t in range(TPG):
                    use = U["o", t // 2]
                    if t != 1:
                        ring.free(pe, g, use)
                    last = mm3(pe, banks[:, use % DEPTH, (t % 2) * D:(t % 2 + 1) * D],
                               [(y_hi[:, k, t * P:(t + 1) * P], y_lo[:, k, t * P:(t + 1) * P]) for k in range(IT)],
                               [part(OUT0, k, D, 0, D) for k in range(IT)])
                    if t == 1:
                        last.then_inc(ring.done, 1)
                last.then_inc(ring.done, 1 + PADS)

            pe.sem_inc(ring.done, ring.n)
            pe.wait_ge(w_in, W_ALL)
            pe.wait_ge(w_in_split, 1)
            stage_x(0, ring.count("P", B0, A0))
            stage_a(0, ring.count("P", C0, ring.n))
            pe.wait_ge(w_split, 2)
            with pe.Fori(1, NG) as g:
                stage_x(g)
                stage_b(g)
                stage_a(g)
                stage_c(g)
            ring.alone(NG, B0)
            stage_b(NG, ring.count("P", A0, C0))
            stage_c(NG)
            ring.alone(None, 0)

        @block.scalar
        def _(act):
            def read(g, name, arg, out, func=ACT.Identity, bias=0.0, scale=1.0, left_out=0):
                ring.filled(act, g, U[name, arg])
                act.activation(out, bank(name, arg)[:, 0:GT], func, bias=bias, scale=scale).then_inc(
                    ring.sems["A"], 1 + left_out)

            def stage_x(g, left_out=0):
                for k in range(KT):
                    read(g, "x", k, x_hi[:, k, :], left_out=left_out if k == KT - 1 else 0)

            def stage_a(g):
                for f in range(IT):
                    ring.filled(act, g, U["u", f])
                    act.activation(u[:, f, :, DC - 1:], bank("u", f)[:, 0:GT].rearrange("p (b t) -> p b t", b=GB),
                                   ACT.Identity, bias=b_in[:, f:f + 1]).then_inc(ring.sems["A"], 1)
                for f in range(IT):
                    act.wait_ge(conv_chain, DC * (IT * g + f + 1))
                    act.activation(uc_hi[:, f, :], conv[:, f, :], ACT.Silu).then_inc(uc_ready, 1)
                    act.activation(conv[:, f, :], conv[:, f, :], ACT.Silu).then_inc(uc_ready, 1)
                    if f == 0:
                        act.wait_ge(y_ready, IT * g + 1)
                    read(g, "g", f, gate[:, f, :], ACT.Tanh, b_gate[:, f:f + 1], 0.5)

            def y_high(g, f):
                act.wait_ge(y_ready, IT * (g - 1) + f + 2)
                act.activation(y_hi[:, f, :], y[:, f, :], ACT.Identity).then_inc(yh_ready, 1)

            def stage_b(g, left_out=0):
                for f in range(IT):
                    ring.filled(act, g, U["b", f])
                    act.wait_ge(state_ready, IT * (g - 1) + f + 1)
                    act.activation(bt[:, f % 2, :], bank("b", f)[:, 0:GT], ACT.Identity,
                                   bias=b_bc[:, f:f + 1]).then_inc(
                        ring.sems["A"], 1 + (left_out if f == IT - 1 else 0))
                    if f:
                        y_high(g, f - 1)
                y_high(g, IT - 1)

            ring.credit(act, "A")
            act.wait_ge(w_in, W_ALL)
            act.activation(decay1[:, :], log_decay[:, :], ACT.Tanh, scale=-0.5).then_inc(decay_act, 1)
            act.activation(w_hi[:, 0:IN], w_raw[:, 0:IN], ACT.Identity).then_inc(w_hi_ready, 1)
            act.wait_ge(w_rest_in, 16)
            act.activation(w_hi[:, IN:OUT0], w_raw[:, IN:OUT0], ACT.Identity).then_inc(w_hi_ready, 1)
            act.activation(w_hi[:, OUT0:], w_raw[:, OUT0:], ACT.Identity, scale=0.5).then_inc(w_hi_ready, 1)
            norm.scalar(act)
            act.wait_ge(tables, 1)
            stage_x(0, ring.count("A", B0, A0))
            stage_a(0)
            with act.Fori(1, NG) as g:
                stage_x(g)
                stage_b(g)
                stage_a(g)
            ring.alone(NG, B0)
            stage_b(NG, ring.count("A", A0, C0))
            ring.alone(None, 0)

        @block.vector
        def _(dve):
            def layernorm(g):
                for t in range(TPG):
                    norm.apply(dve, xn[:, t, :], g * TPG + t).then_inc(xn_ready, 1)

            def stage_x(g, left_out=0):
                layernorm(g)
                for k in range(KT):
                    ring.copied_by(dve, g, U["x", k], "A")
                    dve.tensor_tensor(x_lo[:, k, :], bank("x", k)[:, 0:GT], x_hi[:, k, :].bitcast(F32),
                                      ALU.subtract).then_inc(
                        ring.sems["D"], 1 + (left_out if k == KT - 1 else 0))

            def stage_a(g):
                for f in range(IT):
                    ring.copied_by(dve, g, U["u", f], "A")
                    out = conv[:, f, :].rearrange("p (b t) -> p b t", b=GB)
                    dve.wait_ge(ucl_ready, IT * g + f + 1)
                    for k in range(DC):
                        n = DC * (IT * g + f) + k
                        tap = u[:, f, :, k:k + S]
                        if k == 0:
                            ins = dve.tensor_scalar(out, tap, conv_w[:, f, 0:1], conv_b[:, f:f + 1], ALU.mult, ALU.add)
                        else:
                            dve.wait_ge(conv_chain, n)
                            ins = dve.scalar_tensor_tensor(out, tap, conv_w[:, f, k:k + 1], out, ALU.mult, ALU.add)
                        ins.then_inc(conv_chain, 1)

            def stage_b(g, left_out=0):
                for f in range(IT):
                    n = IT * (g - 1) + f
                    ring.copied_by(dve, g, U["b", f], "A")
                    dve.tensor_tensor_scan(state[:, f % 2, :], decay[:, f, :], bt[:, f % 2, :], 0.0, ALU.mult,
                                           ALU.add).then_inc(state_ready, 1)
                    ring.filled(dve, g, U["c", f])
                    dve.wait_ge(state_ready, n + 3)
                    if f == 0:
                        dve.wait_ge(yl_ready, IT * (g - 1) + 1)
                    dve.scalar_tensor_tensor(y[:, f, :], bank("c", f)[:, 0:GT], b_bc[:, IT + f:IT + f + 1],
                                             state[:, f % 2, :], ALU.add, ALU.mult).then_inc(
                        ring.sems["D"], 1 + (left_out if f == IT - 1 else 0))
                    ring.copied_by(dve, g, U["c", f], "D")
                    dve.scalar_tensor_tensor(y[:, f, :], gate[:, f, :], 1.0, y[:, f, :], ALU.add,
                                             ALU.mult).then_inc(y_ready, 1)

            def stage_c(g):
                for n in range(2):
                    tiles = slice(2 * n, min(2 * n + 2, TPG))
                    w = tiles.stop - tiles.start
                    ring.filled(dve, g, U["o", n])
                    dve.wait_ge(out_added, 2 * (g - 1) + n + 1)
                    dve.tensor_tensor(outb[:, tiles, :], bank("o", n)[:, 0:w * D].rearrange("p (t d) -> p t d", t=w),
                                      bout[:, :].unsqueeze(1).broadcast_to([P, w, D]),
                                      ALU.add).then_inc(ring.sems["D"], 1)

            ring.credit(dve, "D")
            dve.sem_inc(state_ready, 2)
            dve.sem_inc(y_ready, 1)
            norm.vector(dve)
            dve.wait_ge(w_in, W_ALL)
            dve.wait_ge(w_hi_ready, 3)
            dve.scalar_tensor_tensor(w_lo[:, OUT0:], w_raw[:, OUT0:], 0.5, w_hi[:, OUT0:].bitcast(F32), ALU.mult,
                                     ALU.subtract).then_inc(w_split, 1)
            dve.tensor_scalar(b_gate[:, :], b_in[:, IT:2 * IT], 0.5, None, ALU.mult)
            dve.memset(u[:, :, :, :], 0.0)
            dve.wait_ge(decay_act, 1)
            dve.tensor_scalar(decay2[:, :], decay1[:, :], 0.5, 0.5, ALU.mult, ALU.add).then_inc(ready, 1)
            dve.wait_ge(ready, 1)
            dve.tensor_copy(decay[:, :, :], decay2[:, :].unsqueeze(2).broadcast_to([P, IT, GT])).then_inc(ready, 1)
            dve.wait_ge(ready, 2)
            dve.memset(decay[:, :, 0:GT:S], 0.0).then_inc(tables, 1)
            stage_x(0, ring.count("D", B0, A0) + ring.count("D", C0, ring.n))
            stage_a(0)
            with dve.Fori(1, NG) as g:
                stage_x(g)
                stage_b(g)
                stage_a(g)
                stage_c(g)
            ring.alone(NG, B0)
            stage_b(NG, ring.count("D", A0, C0))
            stage_c(NG)
            ring.alone(None, 0)

        @block.gpsimd
        def _(pool):
            def uc_low(g):
                for f in range(IT):
                    pool.wait_ge(uc_ready, 2 * (IT * g + f) + 2)
                    pool.tensor_tensor(uc_lo[:, f, :], conv[:, f, :], uc_hi[:, f, :].bitcast(F32),
                                       ALU.subtract).then_inc(ucl_ready, 1)

            def y_low(g):
                for f in range(IT):
                    pool.wait_ge(yh_ready, IT * (g - 1) + f + 1)
                    pool.tensor_tensor(y_lo[:, f, :], y[:, f, :], y_hi[:, f, :].bitcast(F32),
                                       ALU.subtract).then_inc(yl_ready, 1)

            def add_out(g):
                for n in range(2):
                    w = min(2, TPG - 2 * n)
                    ring.copied(pool, g, U["o", n])
                    tile = Hs[:, bass.ds((g - 1) * TPG + 2 * n, w), :]
                    pool.tensor_tensor(tile, outb[:, 2 * n:2 * n + w, :], tile, ALU.add).then_inc(out_added, 1)

            pool.sem_inc(out_added, 2)
            pool.sem_inc(yl_ready, 1)
            pool.sem_inc(ucl_ready, IT)
            pool.wait_ge(w_hi_ready, 1)
            pool.tensor_tensor(w_lo[:, 0:IN], w_raw[:, 0:IN], w_hi[:, 0:IN].bitcast(F32),
                               ALU.subtract).then_inc(w_in_split, 1)
            pool.wait_ge(w_hi_ready, 2)
            pool.tensor_tensor(w_lo[:, IN:OUT0], w_raw[:, IN:OUT0], w_hi[:, IN:OUT0].bitcast(F32),
                               ALU.subtract).then_inc(w_split, 1)
            uc_low(0)
            with pool.Fori(1, NG) as g:
                y_low(g)
                uc_low(g)
                add_out(g)
            y_low(NG)
            ring.alone(NG, B0)
            add_out(NG)
            ring.alone(None, 0)



HALF_T = NT // 2
HALF_G = NG // 2
EB = 512
EBT = EB // P
BLOCKS = HALF_T // EBT
LAG = 2


def experts(nc, Hs, dram, tag, NE, R, func, routed_from, out=None):
    ctx = ExitStack()
    with ctx:
        mem = Mem(nc, ctx, tag)
        sb, sem = mem.sb, mem.sem
        norm = Norm(mem, Hs)
        WC = KT * FF + FT * D
        W2 = KT * FF
        PAR = min(NE, 2)
        w_raw = sb("w_raw", [P, WC // 2])
        w_hi = sb("w_hi", [P, PAR, WC], F32R)
        w_lo = sb("w_lo", [P, PAR, WC], F32R)
        r_hi = sb("r_hi", [P, KT, P], F32R)
        r_lo = sb("r_lo", [P, KT, P], F32R)
        r_bias = sb("r_bias", [P, 1])
        b1 = sb("b1", [P, NE, FT])
        b1_now = sb("b1_now", [P, 2, FT])
        b2 = sb("b2", [P, NE, D])
        one = sb("one", [P, 1])
        ident = sb("ident", [P, P])
        shared = sb("shared", [P, TPG * D + GT])
        xn = shared[:, 0:TPG * D].rearrange("p (t d) -> p t d", t=TPG)
        logitsT = shared[:, TPG * D:]
        outb = shared[:, 0:4 * D].rearrange("p (b c) -> p b c", b=2)
        xT_hi = sb("xT_hi", [P, KT, HALF_T * P], F32R)
        xT_lo = sb("xT_lo", [P, KT, HALF_T * P], F32R)
        hid = sb("hid", [P, 2, EB])
        hid_hi = sb("hid_hi", [P, 4, EB], F32R)
        hid_lo = sb("hid_lo", [P, 4, EB], F32R)
        r_raw = hid[:, 0, 0:KT * P].rearrange("p (k m) -> p k m", k=KT)
        logits = sb("logits", [P, HALF_T, R])
        prob = sb("prob", [P, HALF_T, R])
        above = sb("above", [P, HALF_T, R, R])
        rank = sb("rank", [P, HALF_T, R])
        total = sb("total", [P, HALF_T])
        inv = sb("inv", [P, HALF_T])
        weight = sb("weight", [P, HALF_T, NE])
        banks = mem.ps("banks", [P, 4, 512])
        acc = mem.ps("acc", [P, 4, 512])

        XB, LTB, LB = (0, 1), 2, 3
        xT_done = sem("xT_done")
        xT_hi_ready = sem("xT_hi_ready")
        xT_lo_ready = sem("xT_lo_ready")
        lT_done = sem("lT_done")
        lT_ready = sem("lT_ready")
        l_done = sem("l_done")
        l_ready = sem("l_ready")
        w_in = sem("w_in")
        raw_in = sem("raw_in")
        w_hi_ready = sem("w_hi_ready")
        w_split = sem("w_split")
        r_hi_ready = sem("r_hi_ready")
        r_split = sem("r_split")
        xn_ready = sem("xn_ready")
        gate_chain = sem("gate_chain")
        gate_exp = sem("gate_exp")
        b1_ready = sem("b1_ready")
        one_ready = sem("one_ready")
        h_done = sem("h_done")
        h_act = sem("h_act")
        h_lo = sem("h_lo")
        h_used = sem("h_used")
        out_read = sem("out_read")
        out_added = sem("out_added")
        stored = sem("stored")
        USED0 = 2 * BLOCKS * FT + 4

        small = [(r_raw, dram[tag + "_router"]), (r_bias[:, :], dram[tag + "_router_b"]),
                 (b1[:, :, :], dram[tag + "_b1"]), (ident[:, :], dram["ident"]),
                 (b2[:, :, :], dram[tag + "_b2"].broadcast_to([P, NE, D]))]
        GATE_STEPS = 7 if routed_from is not None else 10
        CH = WC // 2
        block = ctx.enter_context(nc.Block())

        def over_experts(eng, half, body):
            if NE == 1:
                body(0, 0, half)
            else:
                with eng.Fori(0, NE // 2) as pair:
                    for par in range(2):
                        body(par, pair * 2 + par, pair * 2 + (half * NE + par))

        @block.sync
        def _(sp):
            for dst, src in small:
                sp.dma_start(dst, src).then_inc(w_in, 16)
            def load(e, n, part):
                sp.wait_ge(w_split, n * 2 + (part + 1))
                sp.dma_start(w_raw[:, :], dram[tag + "_w"][bass.ds(e, 1), :, part * CH:(part + 1) * CH].rearrange(
                    "e p c -> p (e c)")).then_inc(raw_in, 16)

            for half in range(2 if NE > 1 else 1):
                with sp.Fori(0, NE) as e:
                    load(e, e + half * NE, 0)
                    load(e, e + half * NE, 1)
            if out is not None:
                rows = out.rearrange("(t p) d -> p t d", p=P)
                stores = [(0, HALF_T)] + [(HALF_T + EBT * i, HALF_T + EBT * (i + 1)) for i in range(BLOCKS)]
                for n, (t0, t1) in enumerate(stores):
                    sp.wait_ge(out_added, 2 * NE * BLOCKS + 1 if n == 0 else
                               2 * (NE + NE - 1) * BLOCKS + 2 + 2 * n)
                    sp.dma_start(rows[:, t0:t1, :], Hs[:, t0:t1, :]).then_inc(stored, 16)
                sp.wait_ge(stored, 16 * len(stores))

        def constants_in(eng):
            eng.wait_ge(w_in, 16 * len(small))

        @block.gpsimd
        def _(pool):
            def split(slot, e, n):
                pool.wait_ge(h_used, n * (BLOCKS * FT) + (BLOCKS * FT + 4))
                for part in range(2):
                    cols = slice(part * CH, (part + 1) * CH)
                    pool.wait_ge(raw_in, n * 32 + 16 * (part + 1))
                    pool.tensor_tensor(w_hi[:, slot, cols], w_raw[:, :], one[:, 0:1].broadcast_to([P, CH]),
                                       ALU.mult).then_inc(w_hi_ready, 1)
                    pool.wait_ge(w_hi_ready, n * 2 + (part + 1))
                    pool.tensor_tensor(w_lo[:, slot, cols], w_raw[:, :], w_hi[:, slot, cols].bitcast(F32),
                                       ALU.subtract).then_inc(w_split, 1)

            pool.sem_inc(w_split, 1)
            pool.memset(one[:, :], 1.0).then_inc(one_ready, 1)
            pool.wait_ge(one_ready, 1)
            for half in range(2 if NE > 1 else 1):
                over_experts(pool, half, split)

        @block.tensor
        def _(pe):
            def turn_x(g, g0):
                for k in range(KT):
                    pe.wait_ge(xT_lo_ready, g * 2 + (k + 1))
                    if k == 0:
                        pe.wait_ge(xn_ready, g * TPG + TPG)
                    for t in range(TPG):
                        last = pe.transpose(banks[:, XB[k], t * P:(t + 1) * P], xn[:, t, k * P:(k + 1) * P],
                                            ident[:, :])
                    last.then_inc(xT_done, 1)

            def route(g, g0):
                pe.wait_ge(lT_ready, g + 1)
                pe.wait_ge(xT_lo_ready, g * 2 + 4)
                cols = bass.ds(g0 * GT, GT)
                mm3(pe, banks[:, LTB, 0:GT], [(r_hi[:, k, :], r_lo[:, k, :]) for k in range(KT)],
                    [(xT_hi[:, k, cols], xT_lo[:, k, cols]) for k in range(KT)]).then_inc(lT_done, 1)

            def turn_logits(g, g0):
                pe.wait_ge(l_ready, g + 1)
                pe.wait_ge(lT_ready, g + 2)
                for t in range(TPG):
                    last = pe.transpose(banks[:, LB, t * P:(t + 1) * P], logitsT[:, t * P:(t + 1) * P], ident[:, :])
                last.then_inc(l_done, 1)

            def prep(half):
                def step(stage, g0):
                    stage(g0 + half * HALF_G, g0)

                step(turn_x, 0)
                step(turn_x, 1)
                step(route, 0)
                with pe.Fori(2, HALF_G) as g0:
                    step(turn_x, g0)
                    step(route, g0 - 1)
                    step(turn_logits, g0 - 2)
                step(route, HALF_G - 1)
                step(turn_logits, HALF_G - 2)
                step(turn_logits, HALF_G - 1)
                pe.wait_ge(l_ready, half * HALF_G + HALF_G + 1)

            def first(slot, block_no, f):
                cols = bass.ds(block_no * EB, EB)
                mm3(pe, banks[:, f % 4, :],
                    [(w_hi[:, slot, k * FF + f * P:k * FF + (f + 1) * P],
                      w_lo[:, slot, k * FF + f * P:k * FF + (f + 1) * P]) for k in range(KT)],
                    [(xT_hi[:, k, cols], xT_lo[:, k, cols]) for k in range(KT)]).then_inc(h_done, 1)

            def second(slot, n, parity, f):
                pe.wait_ge(h_lo, n * FT + (f + 1 + 2))
                if f == 0:
                    pe.wait_ge(out_read, n * 2 + 2)
                rhs = (w_hi[:, slot, W2 + f * D:W2 + (f + 1) * D], w_lo[:, slot, W2 + f * D:W2 + (f + 1) * D])
                for t in range(EBT):
                    last = mm3(pe, acc[:, 2 * parity + t // 2, (t % 2) * D:(t % 2 + 1) * D],
                               [(hid_hi[:, f % 4, t * P:(t + 1) * P], hid_lo[:, f % 4, t * P:(t + 1) * P])], [rhs],
                               start=f == 0 and t % 2 == 0, stop=f == FT - 1, skip=True)
                last.then_inc(h_used, 1)

            def expert(slot, e, n):
                pe.wait_ge(w_split, n * 2 + 3 if NE > 1 else 3)

                def two_blocks(i, last=False):
                    for j in range(2 * FT):
                        second(slot, n * BLOCKS + i * 2 + j // FT, j // FT, j % FT)
                        ahead = j + LAG
                        if not last or ahead < 2 * FT:
                            first(slot, i * 2 + ahead // FT, ahead % FT)

                for f in range(LAG):
                    first(slot, 0, f)
                with pe.Fori(0, BLOCKS // 2 - 1) as i:
                    two_blocks(i)
                two_blocks(BLOCKS // 2 - 1, True)

            pe.sem_inc(xT_done, 2)
            pe.sem_inc(l_done, 1)
            pe.sem_inc(h_used, USED0)
            pe.wait_ge(w_in, 16 * len(small))
            pe.wait_ge(r_split, 1)
            for half in range(2):
                prep(half)
                over_experts(pe, half, expert)

        @block.scalar
        def _(act):
            def prep(half):
                def high(g0):
                    g = g0 + half * HALF_G
                    for k in range(KT):
                        act.wait_ge(xT_done, g * 2 + (k + 3))
                        constants_in(act)
                        act.activation(xT_hi[:, k, bass.ds(g0 * GT, GT)], banks[:, XB[k], 0:GT],
                                       ACT.Identity).then_inc(xT_hi_ready, 1)

                def read_logitsT(g):
                    act.wait_ge(l_done, g + 1)
                    act.wait_ge(lT_done, g + 1)
                    act.activation(logitsT, banks[:, LTB, 0:GT], ACT.Identity,
                                   bias=r_bias[:, 0:1]).then_inc(lT_ready, 1)

                high(0)
                with act.Fori(1, HALF_G) as g0:
                    high(g0)
                    read_logitsT(g0 + (half * HALF_G - 1))
                read_logitsT(half * HALF_G + HALF_G - 1)

            def expert(slot, e, n):
                act.activation(b1_now[:, slot, :], b1[:, bass.ds(e, 1), :].rearrange("p e f -> p (e f)"),
                               ACT.Identity).then_inc(b1_ready, 1)
                act.wait_ge(b1_ready, n + 1)
                with act.Fori(0, BLOCKS // 2) as i:
                    for j in range(2 * FT):
                        f = j % FT
                        step = n * (BLOCKS * FT) + i * (2 * FT) + j
                        bias = b1_now[:, slot, f:f + 1]
                        act.wait_ge(h_done, step + 1)
                        act.wait_ge(h_used, step + (1 + USED0 - 4))
                        act.activation(hid_hi[:, f % 4, :], banks[:, f % 4, :], func, bias=bias).then_inc(h_act, 1)
                        act.wait_ge(h_lo, step + 1)
                        act.activation(hid[:, f % 2, :], banks[:, f % 4, :], func, bias=bias).then_inc(h_act, 1)

            act.sem_inc(lT_ready, 1)
            norm.scalar(act)
            act.wait_ge(w_in, 16 * len(small))
            act.activation(r_hi[:, :, :], r_raw, ACT.Identity).then_inc(r_hi_ready, 1)
            for half in range(2):
                prep(half)
                act.wait_ge(gate_chain, half * GATE_STEPS + 2)
                act.activation(prob[:, :, :], logits[:, :, :], ACT.Exp).then_inc(gate_exp, 1)
                over_experts(act, half, expert)

        @block.vector
        def _(dve):
            def prep(half):
                if half:
                    dve.wait_ge(out_added, NE * BLOCKS * 2 + 1)

                def layernorm(g0):
                    g = g0 + half * HALF_G
                    dve.wait_ge(xT_done, g * 2 + 2)
                    for t in range(TPG):
                        norm.apply(dve, xn[:, t, :], g * TPG + t).then_inc(xn_ready, 1)

                def low(g0):
                    g = g0 + half * HALF_G
                    for k in range(KT):
                        cols = bass.ds(g0 * GT, GT)
                        dve.wait_ge(xT_hi_ready, g * 2 + (k + 1))
                        dve.tensor_tensor(xT_lo[:, k, cols], banks[:, XB[k], 0:GT], xT_hi[:, k, cols].bitcast(F32),
                                          ALU.subtract).then_inc(xT_lo_ready, 1)

                def read_logits(g0):
                    dve.wait_ge(l_done, g0 + (half * HALF_G + 2))
                    dve.tensor_scalar(logits[:, bass.ds(g0 * TPG, TPG), :],
                                      banks[:, LB, 0:GT].rearrange("p (t m) -> p t m", t=TPG)[:, :, 0:R],
                                      1.0, None, ALU.mult).then_inc(l_ready, 1)

                layernorm(0)
                for g0 in range(2):
                    layernorm(g0 + 1)
                    low(g0)
                with dve.Fori(2, HALF_G - 1) as g0:
                    layernorm(g0 + 1)
                    low(g0)
                    read_logits(g0 - 2)
                low(HALF_G - 1)
                for g0 in range(HALF_G - 3, HALF_G):
                    read_logits(g0)

            def gates(half):
                base = half * GATE_STEPS

                def over_classes(v):
                    return v.unsqueeze(2).broadcast_to([P, HALF_T, R])

                dve.wait_ge(l_ready, half * HALF_G + HALF_G + 1)
                dve.reduce_max(total[:, :], logits[:, :, :], AX.X).then_inc(gate_chain, 1)
                dve.wait_ge(gate_chain, base + 1)
                dve.tensor_tensor(logits[:, :, :], logits[:, :, :], over_classes(total[:, :]),
                                  ALU.subtract).then_inc(gate_chain, 1)
                dve.wait_ge(gate_exp, half + 1)
                dve.reduce_sum(total[:, :], prob[:, :, :], AX.X).then_inc(gate_chain, 1)
                dve.wait_ge(gate_chain, base + 3)
                dve.reciprocal(inv[:, :], total[:, :]).then_inc(gate_chain, 1)
                dve.wait_ge(gate_chain, base + 4)
                dve.tensor_tensor(prob[:, :, :], prob[:, :, :], over_classes(inv[:, :]), ALU.mult).then_inc(gate_chain, 1)
                dve.wait_ge(gate_chain, base + 5)
                for c in range(R):
                    for lo, hi, op in ((0, c, ALU.is_ge), (c + 1, R, ALU.is_gt)):
                        if lo < hi:
                            last = dve.tensor_tensor(above[:, :, c, lo:hi], prob[:, :, lo:hi],
                                                     prob[:, :, c:c + 1].broadcast_to([P, HALF_T, hi - lo]), op)
                last.then_inc(gate_chain, 1)
                dve.wait_ge(gate_chain, base + 6)
                dve.reduce_sum(rank[:, :, :], above[:, :, :, :], AX.X).then_inc(gate_chain, 1)
                dve.wait_ge(gate_chain, base + 7)
                if routed_from is not None:
                    dve.memset(weight[:, :, 0:routed_from], 1.0 / routed_from)
                    dve.scalar_tensor_tensor(weight[:, :, routed_from:], rank[:, :, :], 2.0, prob[:, :, :],
                                             ALU.is_lt, ALU.mult).then_inc(out_added, 1)
                else:
                    dve.scalar_tensor_tensor(prob[:, :, :], rank[:, :, :], 2.0, prob[:, :, :], ALU.is_lt,
                                             ALU.mult).then_inc(gate_chain, 1)
                    dve.wait_ge(gate_chain, base + 8)
                    dve.reduce_sum(total[:, :], prob[:, :, :], AX.X).then_inc(gate_chain, 1)
                    dve.wait_ge(gate_chain, base + 9)
                    dve.reciprocal(inv[:, :], total[:, :]).then_inc(gate_chain, 1)
                    dve.wait_ge(gate_chain, base + 10)
                    dve.tensor_tensor(weight[:, :, 0], total[:, :], inv[:, :], ALU.mult).then_inc(out_added, 1)

            def expert(slot, e, n, half):
                def read_out(i, bank):
                    dve.wait_ge(h_used, n * (BLOCKS * FT) + i * (2 * FT) + (bank // 2 + 1) * FT + USED0)
                    bias = b2[:, bass.ds(e, 1), :] if NE > 1 else b2[:, 0:1, :]
                    dve.tensor_tensor(outb[:, bank % 2, :].rearrange("p (t d) -> p t d", t=2),
                                      acc[:, bank, :].rearrange("p (t d) -> p t d", t=2),
                                      bias.broadcast_to([P, 2, D]), ALU.add).then_inc(out_read, 1)

                def add_to_h(i, bank):
                    dve.wait_ge(out_read, n * (2 * BLOCKS) + i * 4 + (bank + 1 + 4))
                    dve.wait_ge(out_added, n * (2 * BLOCKS) + i * 4 + (bank + 1 + half))
                    for t in range(2):
                        tile = i * (2 * EBT) + (2 * bank + t)
                        h = Hs[:, bass.ds(tile + half * HALF_T, 1), :].rearrange("p t d -> p (t d)")
                        wt = weight[:, bass.ds(tile, 1), bass.ds(e, 1) if NE > 1 else slice(0, 1)].rearrange(
                            "p t e -> p (t e)")
                        last = dve.scalar_tensor_tensor(h, outb[:, bank % 2, t * D:(t + 1) * D], wt, h,
                                                        ALU.mult, ALU.add)
                    last.then_inc(out_added, 1)

                def two_blocks(i, first=False):
                    for j in range(2 * FT):
                        step = n * (BLOCKS * FT) + i * (2 * FT) + j
                        dve.wait_ge(h_act, step * 2 + 2)
                        dve.tensor_tensor(hid_lo[:, j % 4, :], hid[:, j % 2, :], hid_hi[:, j % 4, :].bitcast(F32),
                                          ALU.subtract).then_inc(h_lo, 1)
                        if j in (2, 3) and not first:
                            read_out(i - 1, j)
                        if j in (4, 5) and not first:
                            add_to_h(i - 1, j - 2)
                        if j - FT in (2, 3):
                            read_out(i, j - FT - 2)
                        if j - FT in (4, 5):
                            add_to_h(i, j - FT - 4)

                two_blocks(0, True)
                with dve.Fori(1, BLOCKS // 2) as i:
                    two_blocks(i)
                for bank in (2, 3):
                    read_out(BLOCKS // 2 - 1, bank)
                for bank in (2, 3):
                    add_to_h(BLOCKS // 2 - 1, bank)

            dve.sem_inc(xT_lo_ready, 2)
            dve.sem_inc(l_ready, 1)
            dve.sem_inc(h_lo, 2)
            dve.sem_inc(out_read, 4)
            norm.vector(dve)
            dve.memset(above[:, :, :, :].rearrange("p t a b -> p t (a b)")[:, :, 0:R * R:R + 1], 0.0)
            dve.wait_ge(r_hi_ready, 1)
            dve.tensor_tensor(r_lo[:, :, :], r_raw, r_hi[:, :, :].bitcast(F32), ALU.subtract).then_inc(r_split, 1)
            for half in range(2):
                prep(half)
                gates(half)
                over_experts(dve, half, lambda slot, e, n: expert(slot, e, n, half))



def build(nc, dram, out):
    ctx = ExitStack()
    with ctx:
        Hs = ctx.enter_context(nc.sbuf_tensor("residual", [P, NT, D], F32))
        attention(nc, Hs, dram, False)
        recurrence(nc, Hs, dram)
        experts(nc, Hs, dram, "moe", SHARED + ROUTED, ROUTED, ACT.Relu, SHARED)
        attention(nc, Hs, dram, True)
        experts(nc, Hs, dram, "ffn", 1, CLASSES, ACT.Gelu_apprx_tanh, None, out)


def kernel(**inputs):
    import numpy as np
    import concourse.bacc as bacc
    from concourse.bass_utils import run_bass_kernel_spmd as run

    a = {k: np.asarray(v) for k, v in inputs.items()}

    def rows(w):
        return w.reshape(w.shape[0] // P, P, w.shape[1]).transpose(1, 0, 2)

    arrays = {}
    x = a["x"].reshape(NG, GB, M3, 4, KT, P)
    arrays["x"] = x.transpose(0, 5, 4, 3, 1, 2).reshape(NG, P, KT, 4, GB * M3)
    arrays["w_tok"] = rows(np.concatenate([a["L0_tok_Wqkv"].T, a["L0_tok_Wproj"].T], axis=1))
    arrays["ident"] = np.eye(P, dtype=np.float32)
    even = (np.arange(P) // DH % 2 == 0)
    for name, scale in (("masks_tok", D ** -0.5), ("masks_rel", DH ** -0.5)):
        arrays[name] = np.stack([even, ~even], axis=1).astype(np.float32) * np.float32(scale)
    arrays["w_rel"] = rows(np.concatenate([a[f"L1_attn_{n}"].T for n in ("Wq", "Wk", "Wv", "Wo")], axis=1))
    arrays["rel_kT"] = a["L1_attn_rel_k_emb"].T
    arrays["rel_v"] = a["L1_attn_rel_v_emb"]
    arrays["rel_v0_col"] = np.tile(a["L1_attn_rel_v_emb"][0], P // DH).reshape(P, 1)
    arrays["b_o"] = a["L1_attn_b_o"].reshape(1, D)
    w_in, w_bc, w_out = (rows(a[f"L0_attn_{n}"]).reshape(P, -1) for n in ("W_in", "W_bc", "W_out"))
    arrays["w_rc"] = np.concatenate([w_in, w_bc, w_out], axis=1)

    def column(v):
        return v.reshape(-1, P).T

    arrays["rc_b_in"] = column(a["L0_attn_b_in"])
    arrays["rc_conv_w"] = a["L0_attn_conv_w"].reshape(IT, P, DC).transpose(1, 0, 2)
    arrays["rc_conv_b"] = column(a["L0_attn_conv_b"])
    arrays["rc_b_bc"] = column(a["L0_attn_b_bc"])
    arrays["rc_log_decay"] = column(a["L0_attn_log_decay"])
    arrays["rc_b_out"] = a["L0_attn_b_out"].reshape(1, D)

    def expert_arrays(tag, w1, b1, w2, b2, router, router_b):
        n = w1.shape[0]
        arrays[tag + "_w"] = np.concatenate(
            [w1.reshape(n, KT, P, FF).transpose(0, 2, 1, 3).reshape(n, P, KT * FF),
             w2.reshape(n, FT, P, D).transpose(0, 2, 1, 3).reshape(n, P, FT * D)], axis=2)
        arrays[tag + "_b1"] = b1.reshape(n, FT, P).transpose(2, 0, 1)
        arrays[tag + "_b2"] = b2.reshape(1, n, D)
        arrays[tag + "_router"] = rows(np.pad(router, ((0, 0), (0, P - router.shape[1]))))
        arrays[tag + "_router_b"] = np.pad(router_b, (0, P - router_b.shape[0])).reshape(P, 1)

    def both(suffix):
        return np.concatenate([a["L0_ffn_s" + suffix], a["L0_ffn_r" + suffix]])

    expert_arrays("moe", both("w1"), both("b1"), both("w2"), both("b2"), a["L0_ffn_gate_w"], a["L0_ffn_gate_b"])
    expert_arrays("ffn", a["L1_ffn_w1"][None], a["L1_ffn_b1"][None], a["L1_ffn_w2"][None], a["L1_ffn_b2"][None],
                  a["L1_ffn_router_w"], np.zeros(CLASSES, np.float32))
    nc = bacc.Bacc("TRN2", target_bir_lowering=False, num_devices=1)
    arrays = {f"in_{k}": np.ascontiguousarray(v) for k, v in arrays.items()}
    dram = {k[3:]: nc.dram_tensor(k, v.shape, mybir.dt.from_np(v.dtype), kind="ExternalInput").ap()
            for k, v in arrays.items()}
    for name in ("skew_s", "skew_p"):
        dram[name] = nc.dram_tensor(name, (TPG, P, H, ROW), F32, kind="Internal").ap()
    out = nc.dram_tensor("out", (B * S, D), F32, kind="ExternalOutput").ap()
    build(nc, dram, out)
    got = run(nc, [arrays], core_ids=[0])
    return got.results[0]["out"].reshape(B, S, D)
```
